# Optimizing a Trainium2 kernel written in Bass

```python
import numpy as np
import jax
import jax.numpy as jnp

def _softmax(x, axis=-1):
    return jax.nn.softmax(x, axis=axis)

def _gelu(x):
    return jax.nn.gelu(x, approximate=True)

def _silu(x):
    return jax.nn.silu(x)

def _sigmoid(x):
    return jax.nn.sigmoid(x)

def _layernorm(x, axis=-1, eps=1e-05):
    m = jnp.mean(x, axis=axis, keepdims=True)
    v = jnp.var(x, axis=axis, keepdims=True)
    return (x - m) / jnp.sqrt(v + eps)

def _scatter_add(tgt, idx, src, axis=0):
    return tgt.at[idx].add(src)

def _segment_sum(src, seg, n):
    return jax.ops.segment_sum(src, seg, n)
kernel_name = 'mk_gnn_preln_d4_gnn_r32_a3452c'

def setup_inputs(seed: int=0):
    np.random.seed(seed)
    _w = jnp.asarray

    def _rec_inputs():
        import jax
        import jax.numpy as jnp
        _gk = jax.random.key(seed)
        x = -0.001003 + 1 * jax.random.normal(jax.random.fold_in(_gk, 1), (96, 512), jnp.float32)
        src = jax.random.randint(jax.random.fold_in(_gk, 2), (1536,), 0, 96, jnp.int32)
        dst = jax.random.randint(jax.random.fold_in(_gk, 3), (1536,), 0, 96, jnp.int32)
        _o = jnp.argsort(dst, stable=True)
        src = src[_o]
        dst = dst[_o]
        edge_type_2 = jax.random.randint(jax.random.fold_in(_gk, 13), (1536,), 0, 2, jnp.int32)
        edge_type_8 = jax.random.randint(jax.random.fold_in(_gk, 14), (1536,), 0, 8, jnp.int32)
        edge_weight = jax.random.uniform(jax.random.fold_in(_gk, 15), (1536,), jnp.float32, 0.0, 0.999998)
        return (x, src, dst, edge_type_2, edge_type_8, edge_weight)
    x, src, dst, edge_type_2, edge_type_8, edge_weight = _rec_inputs()

    def _L0_gnn_setup():
        import jax, jax.numpy as jnp
        import numpy as np
        H = 8
        D = 64
        N = 96
        IN_DIM = 512
        E = 3072
        key = jax.random.key(seed)
        ks = jax.random.split(key, 8)
        x = jax.random.normal(ks[0], (N, IN_DIM), dtype=jnp.float32)
        edge_index = jax.random.randint(ks[1], (2, E), 0, N, dtype=jnp.int64)
        s = 1.0 / np.sqrt(IN_DIM)
        Wq = jax.random.normal(ks[2], (IN_DIM, H * D), dtype=jnp.float32) * s
        Wk = jax.random.normal(ks[3], (IN_DIM, H * D), dtype=jnp.float32) * s
        Wv = jax.random.normal(ks[4], (IN_DIM, H * D), dtype=jnp.float32) * s
        bq = jax.random.normal(ks[5], (H * D,), dtype=jnp.float32) * 0.01
        bk = jax.random.normal(ks[6], (H * D,), dtype=jnp.float32) * 0.01
        bv = jax.random.normal(ks[7], (H * D,), dtype=jnp.float32) * 0.01
        return {'x': x, 'edge_index': edge_index, 'Wq': Wq, 'Wk': Wk, 'Wv': Wv, 'bq': bq, 'bk': bk, 'bv': bv}
    _L0_gnn_all = _L0_gnn_setup()
    _L0_gnn_in = {k: v for k, v in _L0_gnn_all.items() if k in ('Wq', 'Wk', 'Wv', 'bq', 'bk', 'bv')}
    del _L0_gnn_all

    def _L1_gnn_setup():
        import jax, jax.numpy as jnp
        import numpy as np
        NUM_RELATIONS = 2
        NUM_BASES = 30
        HIDDEN = 512
        N_NODES = 10000
        N_EDGES = 5000

        def rgcn_gate_layer(x, row, col, edge_type, basis, att, gate_w, root, bias):
            H = x.shape[1]
            w = jnp.einsum('rb,bio->rio', att, basis)
            x_j = x[col]
            msgs = []
            for r in range(NUM_RELATIONS):
                gate = jax.nn.sigmoid(x_j @ gate_w[r, :, 0])
                msgs.append(gate[:, None] * x_j @ w[r])
            msg = jnp.where((edge_type == 0)[:, None], msgs[0], msgs[1])
            agg = jax.ops.segment_sum(msg, row, num_segments=x.shape[0])
            return agg + x @ root + bias
        key = jax.random.key(seed)
        ks = jax.random.split(key, 16)
        H, R, B = (HIDDEN, NUM_RELATIONS, NUM_BASES)
        bound = 1.0 / np.sqrt(B * H)
        u = lambda k, shape: jax.random.uniform(k, shape, jnp.float32, -bound, bound)
        inp = {'x': jax.random.normal(ks[0], (N_NODES, H), jnp.float32), 'edge_index': jax.random.randint(ks[1], (2, N_EDGES), 0, N_NODES, jnp.int32), 'edge_type': jax.random.randint(ks[2], (N_EDGES,), 0, R, jnp.int32), 'basis1': u(ks[3], (B, H, H)), 'att1': u(ks[4], (R, B)), 'gate_w1': u(ks[5], (R, H, 1)), 'root1': u(ks[6], (H, H)), 'bias1': u(ks[7], (H,)), 'basis2': u(ks[8], (B, H, H)), 'att2': u(ks[9], (R, B)), 'gate_w2': u(ks[10], (R, H, 1)), 'root2': u(ks[11], (H, H)), 'bias2': u(ks[12], (H,))}
        return inp
    _L1_gnn_all = _L1_gnn_setup()
    _L1_gnn_in = {k: v for k, v in _L1_gnn_all.items() if k in ('basis1', 'att1', 'gate_w1', 'root1', 'bias1', 'basis2', 'att2', 'gate_w2', 'root2', 'bias2')}
    del _L1_gnn_all

    def _L2_gnn_setup():
        import jax, jax.numpy as jnp
        import numpy as np
        N = 10000
        E = 5000
        H = 4
        C = 256
        D_IN = 512
        D_OUT = 512
        NEG_SLOPE = 0.2

        def gat_conv(x, src, dst, W, a_src, a_dst, bias):
            n = x.shape[0]
            h = (x @ W).reshape(n, H, C)
            al_s = jnp.einsum('nhc,hc->nh', h, a_src)
            al_d = jnp.einsum('nhc,hc->nh', h, a_dst)
            e = jax.nn.leaky_relu(al_s[src] + al_d[dst], NEG_SLOPE)
            emax = jax.ops.segment_max(e, dst, num_segments=n)
            w = jnp.exp(e - emax[dst])
            denom = jax.ops.segment_sum(w, dst, num_segments=n)
            alpha = w / denom[dst]
            out = jax.ops.segment_sum(h[src] * alpha[:, :, None], dst, num_segments=n)
            return out.reshape(n, H * C) + bias
        key = jax.random.key(seed)
        ks = jax.random.split(key, 13)
        s = 0.05
        return {'x': jax.random.normal(ks[0], (N, D_IN), jnp.float32), 'edge_index': jax.random.randint(ks[1], (2, E), 0, N, dtype=jnp.int32), 'W1': jax.random.normal(ks[2], (D_IN, H * C), jnp.float32) * s, 'a_src1': jax.random.normal(ks[3], (H, C), jnp.float32) * s, 'a_dst1': jax.random.normal(ks[4], (H, C), jnp.float32) * s, 'b1': jnp.zeros((H * C,), jnp.float32), 'W2': jax.random.normal(ks[5], (H * C, H * C), jnp.float32) * s, 'a_src2': jax.random.normal(ks[6], (H, C), jnp.float32) * s, 'a_dst2': jax.random.normal(ks[7], (H, C), jnp.float32) * s, 'b2': jnp.zeros((H * C,), jnp.float32), 'Wfc': jax.random.normal(ks[8], (H * C, D_OUT), jnp.float32) * s, 'bfc': jnp.zeros((D_OUT,), jnp.float32)}
    _L2_gnn_all = _L2_gnn_setup()
    _L2_gnn_in = {k: v for k, v in _L2_gnn_all.items() if k in ('W1', 'a_src1', 'a_dst1', 'b1', 'W2', 'a_src2', 'a_dst2', 'b2', 'Wfc', 'bfc')}
    del _L2_gnn_all

    def _L3_gnn_setup():
        import jax, jax.numpy as jnp
        import numpy as np
        N_NODES = 625
        N_EDGES = 10000
        D = 512
        NUM_RELS = 8
        NUM_BASES = 4

        def _rel_graph_conv(h, src, dst, etypes, norm, basis, comp, bias, loop_w, apply_relu):
            n = h.shape[0]
            hb = jnp.einsum('nd,bdo->bno', h, basis)
            coef = comp[etypes]
            m = coef[:, 0, None] * hb[0][src]
            for b in range(1, basis.shape[0]):
                m = m + coef[:, b, None] * hb[b][src]
            m = m * norm[:, None]
            agg = jax.ops.segment_sum(m, dst, num_segments=n)
            out = agg + bias + h @ loop_w
            if apply_relu:
                out = jax.nn.relu(out)
            return out
        key = jax.random.key(seed)
        ks = jax.random.split(key, 16)
        inp = {'emb': jax.random.normal(ks[0], (N_NODES, D), dtype=jnp.float32), 'src': jax.random.randint(ks[1], (N_EDGES,), 0, N_NODES), 'dst': jax.random.randint(ks[2], (N_EDGES,), 0, N_NODES), 'etypes': jax.random.randint(ks[3], (N_EDGES,), 0, NUM_RELS), 'edge_norm': jax.random.uniform(ks[4], (N_EDGES,), dtype=jnp.float32)}
        s = 1.0 / np.sqrt(D)
        inp['basis0'] = jax.random.normal(ks[5], (NUM_BASES, D, D), dtype=jnp.float32) * s
        inp['comp0'] = jax.random.normal(ks[6], (NUM_RELS, NUM_BASES), dtype=jnp.float32)
        inp['bias0'] = jnp.zeros((D,), dtype=jnp.float32)
        inp['loop0'] = jax.random.normal(ks[7], (D, D), dtype=jnp.float32) * s
        inp['basis1'] = jax.random.normal(ks[8], (NUM_BASES, D, D), dtype=jnp.float32) * s
        inp['comp1'] = jax.random.normal(ks[9], (NUM_RELS, NUM_BASES), dtype=jnp.float32)
        inp['bias1'] = jnp.zeros((D,), dtype=jnp.float32)
        inp['loop1'] = jax.random.normal(ks[10], (D, D), dtype=jnp.float32) * s
        return inp
    _L3_gnn_all = _L3_gnn_setup()
    _L3_gnn_in = {k: v for k, v in _L3_gnn_all.items() if k in ('basis0', 'comp0', 'bias0', 'loop0', 'basis1', 'comp1', 'bias1', 'loop1')}
    del _L3_gnn_all
    return {'x': x, 'src': src, 'dst': dst, 'edge_type_2': edge_type_2, 'edge_type_8': edge_type_8, 'edge_weight': edge_weight, 'L0_gnn_Wq': _L0_gnn_in['Wq'], 'L0_gnn_Wk': _L0_gnn_in['Wk'], 'L0_gnn_Wv': _L0_gnn_in['Wv'], 'L0_gnn_bq': _L0_gnn_in['bq'], 'L0_gnn_bk': _L0_gnn_in['bk'], 'L0_gnn_bv': _L0_gnn_in['bv'], 'L1_gnn_basis1': _L1_gnn_in['basis1'], 'L1_gnn_att1': _L1_gnn_in['att1'], 'L1_gnn_gate_w1': _L1_gnn_in['gate_w1'], 'L1_gnn_root1': _L1_gnn_in['root1'], 'L1_gnn_bias1': _L1_gnn_in['bias1'], 'L1_gnn_basis2': _L1_gnn_in['basis2'], 'L1_gnn_att2': _L1_gnn_in['att2'], 'L1_gnn_gate_w2': _L1_gnn_in['gate_w2'], 'L1_gnn_root2': _L1_gnn_in['root2'], 'L1_gnn_bias2': _L1_gnn_in['bias2'], 'L2_gnn_W1': _L2_gnn_in['W1'], 'L2_gnn_a_src1': _L2_gnn_in['a_src1'], 'L2_gnn_a_dst1': _L2_gnn_in['a_dst1'], 'L2_gnn_b1': _L2_gnn_in['b1'], 'L2_gnn_W2': _L2_gnn_in['W2'], 'L2_gnn_a_src2': _L2_gnn_in['a_src2'], 'L2_gnn_a_dst2': _L2_gnn_in['a_dst2'], 'L2_gnn_b2': _L2_gnn_in['b2'], 'L2_gnn_Wfc': _L2_gnn_in['Wfc'], 'L2_gnn_bfc': _L2_gnn_in['bfc'], 'L3_gnn_basis0': _L3_gnn_in['basis0'], 'L3_gnn_comp0': _L3_gnn_in['comp0'], 'L3_gnn_bias0': _L3_gnn_in['bias0'], 'L3_gnn_loop0': _L3_gnn_in['loop0'], 'L3_gnn_basis1': _L3_gnn_in['basis1'], 'L3_gnn_comp1': _L3_gnn_in['comp1'], 'L3_gnn_bias1': _L3_gnn_in['bias1'], 'L3_gnn_loop1': _L3_gnn_in['loop1']}

def reference(x, src, dst, edge_type_2, edge_type_8, edge_weight, L0_gnn_Wq, L0_gnn_Wk, L0_gnn_Wv, L0_gnn_bq, L0_gnn_bk, L0_gnn_bv, L1_gnn_basis1, L1_gnn_att1, L1_gnn_gate_w1, L1_gnn_root1, L1_gnn_bias1, L1_gnn_basis2, L1_gnn_att2, L1_gnn_gate_w2, L1_gnn_root2, L1_gnn_bias2, L2_gnn_W1, L2_gnn_a_src1, L2_gnn_a_dst1, L2_gnn_b1, L2_gnn_W2, L2_gnn_a_src2, L2_gnn_a_dst2, L2_gnn_b2, L2_gnn_Wfc, L2_gnn_bfc, L3_gnn_basis0, L3_gnn_comp0, L3_gnn_bias0, L3_gnn_loop0, L3_gnn_basis1, L3_gnn_comp1, L3_gnn_bias1, L3_gnn_loop1):
    import jax
    import jax.numpy as jnp

    def _L0_gnn_ref(x, edge_index, Wq, Wk, Wv, bq, bk, bv):
        import jax, jax.numpy as jnp
        import numpy as np
        H = 8
        D = 64
        N = 96
        IN_DIM = 512
        E = 3072

        def proj(W, b):
            return (x @ W + b).reshape(N, H, D).transpose(1, 0, 2)
        q, k, v = (proj(Wq, bq), proj(Wk, bk), proj(Wv, bv))
        scores = jnp.einsum('hnd,hmd->hnm', q, k) / jnp.sqrt(jnp.float32(D))
        src, dst = (edge_index[0], edge_index[1])
        masked = jnp.zeros_like(scores).at[-1, src, dst].set(scores[-1, src, dst])
        att = jax.nn.softmax(masked, axis=-1)
        out = jnp.einsum('hnm,hmd->hnd', att, v)
        return out.transpose(1, 0, 2).reshape(N, H * D)

    def _L1_gnn_ref(x, edge_index, edge_type, basis1, att1, gate_w1, root1, bias1, basis2, att2, gate_w2, root2, bias2):
        import jax, jax.numpy as jnp
        import numpy as np
        NUM_RELATIONS = 2
        NUM_BASES = 30
        HIDDEN = 512
        N_NODES = 10000
        N_EDGES = 5000

        def rgcn_gate_layer(x, row, col, edge_type, basis, att, gate_w, root, bias):
            H = x.shape[1]
            w = jnp.einsum('rb,bio->rio', att, basis)
            x_j = x[col]
            msgs = []
            for r in range(NUM_RELATIONS):
                gate = jax.nn.sigmoid(x_j @ gate_w[r, :, 0])
                msgs.append(gate[:, None] * x_j @ w[r])
            msg = jnp.where((edge_type == 0)[:, None], msgs[0], msgs[1])
            agg = jax.ops.segment_sum(msg, row, num_segments=x.shape[0])
            return agg + x @ root + bias
        row, col = (edge_index[0], edge_index[1])
        h = jax.nn.relu(rgcn_gate_layer(x, row, col, edge_type, basis1, att1, gate_w1, root1, bias1))
        out = rgcn_gate_layer(h, row, col, edge_type, basis2, att2, gate_w2, root2, bias2)
        return out

    def _L2_gnn_ref(x, edge_index, W1, a_src1, a_dst1, b1, W2, a_src2, a_dst2, b2, Wfc, bfc):
        import jax, jax.numpy as jnp
        import numpy as np
        N = 10000
        E = 5000
        H = 4
        C = 256
        D_IN = 512
        D_OUT = 512
        NEG_SLOPE = 0.2

        def gat_conv(x, src, dst, W, a_src, a_dst, bias):
            n = x.shape[0]
            h = (x @ W).reshape(n, H, C)
            al_s = jnp.einsum('nhc,hc->nh', h, a_src)
            al_d = jnp.einsum('nhc,hc->nh', h, a_dst)
            e = jax.nn.leaky_relu(al_s[src] + al_d[dst], NEG_SLOPE)
            emax = jax.ops.segment_max(e, dst, num_segments=n)
            w = jnp.exp(e - emax[dst])
            denom = jax.ops.segment_sum(w, dst, num_segments=n)
            alpha = w / denom[dst]
            out = jax.ops.segment_sum(h[src] * alpha[:, :, None], dst, num_segments=n)
            return out.reshape(n, H * C) + bias
        loop = jnp.arange(N, dtype=edge_index.dtype)
        src = jnp.concatenate([edge_index[0], loop])
        dst = jnp.concatenate([edge_index[1], loop])
        h = jax.nn.relu(gat_conv(x, src, dst, W1, a_src1, a_dst1, b1))
        h = jax.nn.relu(gat_conv(h, src, dst, W2, a_src2, a_dst2, b2))
        return h @ Wfc + bfc

    def _L3_gnn_ref(emb, src, dst, etypes, edge_norm, basis0, comp0, bias0, loop0, basis1, comp1, bias1, loop1):
        import jax, jax.numpy as jnp
        import numpy as np
        N_NODES = 625
        N_EDGES = 10000
        D = 512
        NUM_RELS = 8
        NUM_BASES = 4

        def _rel_graph_conv(h, src, dst, etypes, norm, basis, comp, bias, loop_w, apply_relu):
            n = h.shape[0]
            hb = jnp.einsum('nd,bdo->bno', h, basis)
            coef = comp[etypes]
            m = coef[:, 0, None] * hb[0][src]
            for b in range(1, basis.shape[0]):
                m = m + coef[:, b, None] * hb[b][src]
            m = m * norm[:, None]
            agg = jax.ops.segment_sum(m, dst, num_segments=n)
            out = agg + bias + h @ loop_w
            if apply_relu:
                out = jax.nn.relu(out)
            return out
        h = _rel_graph_conv(emb, src, dst, etypes, edge_norm, basis0, comp0, bias0, loop0, True)
        h = _rel_graph_conv(h, src, dst, etypes, edge_norm, basis1, comp1, bias1, loop1, False)
        return h
    edge_index = jnp.stack([src, dst])
    h = jnp.maximum(_layernorm(x, axis=-1), 0.0)
    x = x + _L0_gnn_ref(h, edge_index, L0_gnn_Wq, L0_gnn_Wk, L0_gnn_Wv, L0_gnn_bq, L0_gnn_bk, L0_gnn_bv)
    h = jnp.maximum(_layernorm(x, axis=-1), 0.0)
    x = x + _L1_gnn_ref(h, edge_index, edge_type_2, L1_gnn_basis1, L1_gnn_att1, L1_gnn_gate_w1, L1_gnn_root1, L1_gnn_bias1, L1_gnn_basis2, L1_gnn_att2, L1_gnn_gate_w2, L1_gnn_root2, L1_gnn_bias2)
    h = jnp.maximum(_layernorm(x, axis=-1), 0.0)
    x = x + _L2_gnn_ref(h, edge_index, L2_gnn_W1, L2_gnn_a_src1, L2_gnn_a_dst1, L2_gnn_b1, L2_gnn_W2, L2_gnn_a_src2, L2_gnn_a_dst2, L2_gnn_b2, L2_gnn_Wfc, L2_gnn_bfc)
    h = jnp.maximum(_layernorm(x, axis=-1), 0.0)
    x = x + _L3_gnn_ref(h, src, dst, edge_type_8, edge_weight, L3_gnn_basis0, L3_gnn_comp0, L3_gnn_bias0, L3_gnn_loop0, L3_gnn_basis1, L3_gnn_comp1, L3_gnn_bias1, L3_gnn_loop1)
    return x

_drawn_inputs = setup_inputs


def setup_inputs(seed=0):
    import zlib

    import numpy as np

    out = dict(_drawn_inputs(seed))
    spreads = {'L2_gnn_b1': (0.0, 0.1),
     'L2_gnn_b2': (0.0, 0.1),
     'L2_gnn_bfc': (0.0, 0.1),
     'L3_gnn_bias0': (0.0, 0.268),
     'L3_gnn_bias1': (0.0, 0.8)}
    factors = {'L0_gnn_Wq': 8.0,
     'L0_gnn_Wk': 8.0,
     'L0_gnn_bq': 64.0,
     'L0_gnn_bk': 64.0,
     'L0_gnn_bv': 7.119,
     'L1_gnn_basis1': 8.0,
     'L1_gnn_att1': 8.0,
     'L1_gnn_gate_w1': 8.0,
     'L1_gnn_root1': 8.0,
     'L1_gnn_bias1': 22.475,
     'L1_gnn_basis2': 8.0,
     'L1_gnn_att2': 8.0,
     'L1_gnn_gate_w2': 8.0,
     'L1_gnn_root2': 8.0,
     'L1_gnn_bias2': 8.0,
     'L2_gnn_a_dst1': 64.0,
     'L2_gnn_a_src2': 31.155,
     'L2_gnn_a_dst2': 64.0,
     'L2_gnn_a_src1': 4.185}
    for name, (base, spread) in spreads.items():
        noise = np.random.default_rng([zlib.crc32(name.encode()), seed]).standard_normal(out[name].shape)
        drawn = base * np.exp(spread * noise) if base else spread * noise
        out[name] = jnp.asarray(drawn.astype(out[name].dtype))
    for name, factor in factors.items():
        out[name] = (out[name] * factor).astype(out[name].dtype)
    return out
```

```python
from contextlib import ExitStack

import concourse.bass as bass
from concourse import mybir

F32 = mybir.dt.float32
BF16 = mybir.dt.bfloat16
I32 = mybir.dt.int32
ALU = mybir.AluOpType
ACT = mybir.ActivationFunctionType
X = mybir.AxisListType.X

N = 96
D = 512
E = 1536
P = 128
EC = E // P
KC = D // P
HEADS, HD = 8, 64
NB, NR = 30, 2
BLOCKS = 4
BP = NB * BLOCKS
GROUPS, STEPS = 4, 4
TILE = BLOCKS * GROUPS * STEPS
TILES = D // TILE
HALVES = 2
SLOTS = 8
LOOP_TILES = SLOTS // HALVES
GH, GC = 4, 256
GD = GH * GC
ET, EB = 8, 4
EPS = 1e-5
ABSENT = -1e30

ROW_BV, ROW_L1B, ROW_B1, ROW_B2, ROW_BFC, ROW_L3B, ROW_A = 0, 1, 3, 5, 7, 8, 10
ROWS = 18


def gnn_blocks(nc, io, out):
    with ExitStack() as ctx:
        def sb(name, shape, dt=F32):
            return ctx.enter_context(nc.sbuf_tensor(name, shape, dt))

        def sem(name):
            return ctx.enter_context(nc.semaphore(name))

        ring = sb("ring", [P, SLOTS, 8 * D])
        early = sb("early", [P, 8 * D])
        wv = early[:, 0:4 * D].rearrange("p (k f) -> p k f", k=KC)
        root1 = early[:, 4 * D:8 * D].rearrange("p (k f) -> p k f", k=KC)
        avec = early[0:N, :].rearrange("p (g f) -> p g f", g=4)
        late = sb("late", [P, KC * 5 * N + 128])
        root2 = late[:, 0:4 * D].rearrange("p (k f) -> p k f", k=KC)
        zT = late[:, 0:KC * 5 * N].rearrange("p (k f) -> p k f", k=KC)
        wqk = sb("wqk", [P, 2, KC, HD])
        mixed = sb("mixed", [N, NR, TILES * P])
        gat_h = mixed[:, 0, :]
        gat_o = mixed[:, 1, :]
        yT = sb("yT", [P, TILES, N])
        y_now = sb("y_now", [P, LOOP_TILES, N])
        w_sb = sb("w_sb", [P, 2, D])
        x = sb("x", [N, D])
        h = sb("h", [N, D])
        hT = sb("hT", [P, 8, N])
        v = yT[0:N].rearrange("p t n -> p (t n)")[:, 0:D]
        qk = y_now[0:HD, 0:2, :]
        ident = sb("ident", [P, P])
        iota = sb("iota", [P, N])
        ones = sb("ones", [N, N])
        uniform = sb("uniform", [N, N])
        rows = sb("rows", [ROWS, D])
        bqk = sb("bqk", [1, 2, HD])
        gate_rows = sb("gate_rows", [2 * NR, D])
        gateT = sb("gateT", [P, KC, 2 * NR])
        edge_i = sb("edge_i", [P, 4, EC], I32)
        edge_f = sb("edge_f", [P, 4, EC])
        weight = sb("weight", [P, EC])
        comp = sb("comp", [P, 2, ET * EB])
        att_rows = sb("att_rows", [2 * NR, NB])
        att_p = sb("att_p", [BP, 2 * NR])
        same_block = sb("same_block", [BP, BLOCKS])
        att_w = sb("att_w", [BP, 2, 160])
        edge_area = sb("edge_area", [P, 3 * EC * N // 2])
        hots = edge_area[:].bitcast(BF16).rearrange("p (a e n) -> p a e n", a=3, e=EC)
        src_hot, dst_hot, src_hot0 = hots[:, 0], hots[:, 1], hots[:, 2]
        src_c = sb("src_c", [P, 2, N])
        mix3 = sb("mix3", [N, 2, 5 * N])
        is_rel0 = sb("is_rel0", [P, EC])
        has_edge = sb("has_edge", [N, N])
        relT = sb("relT", [N, NR, N])
        gat_count = sb("gat_count", [N, N])
        absent = sb("absent", [N, N])
        is_type = sb("is_type", [P, EC, ET])
        typed = sb("typed", [P, EC, EB, ET])
        coef = sb("coef", [P, EC, 2, EB])
        work = sb("work", [P, 2, 2 * EB * N])
        score = work[0:N, 0, 0:GH * N].rearrange("p (g s) -> p g s", g=GH)
        score2 = work[0:N, 0, GH * N:2 * GH * N].rearrange("p (g s) -> p g s", g=GH)
        alphaT = work[0:N, 1, 0:GH * N].rearrange("p (g s) -> p g s", g=GH)
        dot_out = [work[0:N, a, c:c + GC] for a, c in ((0, 0), (0, GH * N), (1, GH * N))]
        expand = work[0:2 * NR, 1, GH * N + GC:GH * N + GC + BP].rearrange("p (b k) -> p b k", b=NB)
        al = sb("al", [N, 2, GH])
        stat = sb("stat", [N, 32])
        z_exp = sb("z_exp", [N, NR])
        gate = sb("gate", [N, NR])
        bank = [ctx.enter_context(nc.psum_tensor(f"bank{i}", [P, D], F32)) for i in range(8)]

        W1 = ring[:, 0, :].rearrange("p (k f) -> p k f", k=4)
        W2 = ring[:, 1:3, :].rearrange("p s (k f) -> p (s k) f", k=4)
        Wfc = ring[:, 3, :].rearrange("p (k f) -> p k f", k=8)
        conv_w = [[ring[:, slot, c * 4 * D:(c + 1) * 4 * D].rearrange("p (k f) -> p k f", k=KC) for slot, c in at]
                  for at in (((4, 0), (4, 1), (5, 0), (5, 1), (6, 0)), ((7, 0), (7, 1), (0, 0), (0, 1), (6, 1)))]

        names = """x_in edges_in rel_in wqk_in wv_in bv_in bqk_in rows_in gate_in att_in etype_in weight_in comp_in
            root1_in root2_in w1_in w1b_in w2_in w2b_in wfc_in b0a_in b0b_in loops_in b1a_in b1b_in out_done
            ident_ready iota_ready consts_ready edges_float hots_ready hot0_ready
            half_free w_copied y_ready contracted
            counts_done rel_ready edge_mask gat_mask
            ln_stats ln_var ln_rstd ln_scaled h_ready hT_done hT_ready hT_high_done hT_high_ready
            qk_done qk_ready v_done v_ready scores_done masked max_ready exp_ready att_norm att_turned att_turned_ready
            attn_done x_ready
            expand_ready attp_done attp_ready block_ready attw_zero attw_ready gateT_done gateT_ready
            gates_done z_ready gate_p1 gate_ready mixed_zero mixed_ready yT_done yT_a yT_ready agg_started
            coef_steps coef_ready hot_c_ready hot_w_ready hot_w_used mix_ready
            avec_done avec_ready
            proj_a proj_b h_copied al_ready diag_ready e_done softmax_step s_masked s_exp alpha_ready alpha_done alphaT_ready
            gat_out_a gat_out_b gat_ready_a gat_ready_b
            fc_done zT_done zT_dve zT_act conv_done result_ready""".split()
        s = {n: sem(n) for n in names}
        half_in = [sem(f"half_in{i}") for i in range(SLOTS)]

        block = ctx.enter_context(nc.Block())

        def chunked(w):
            return w.rearrange("(k p) f -> p k f", p=P)

        BN, MEAN, VAR, VAR_EPS, RSTD, NEG_MAX, EXP_SUM, EXP_RCP, NEG_HALF = 0, 6, 7, 10, 11, 8, 9, 12, 16
        GAT_MAX, GAT_SUM, GAT_RCP = 20, 24, 28

        def pick(r):
            return ident[0:ROWS, r:r + 1].broadcast_to([ROWS, N])

        def rstd_pow(pool, n):
            pool.wait_ge(s["consts_ready"], 1)
            pool.wait_ge(s["ln_var"], n)
            nc.gpsimd.tensor_tensor(stat[:, RSTD:RSTD + 1], stat[:, VAR_EPS:VAR_EPS + 1],
                                    stat[:, NEG_HALF:NEG_HALF + 1], ALU.pow).then_inc(s["ln_rstd"], 1)

        def copy_hT_high(act, n):
            act.wait_ge(s["hT_high_done"], n)
            nc.scalar.copy(hT[:, 4:8, :], bank[4][:, 0:4 * N].rearrange("p (k n) -> p k n", k=4)
                           ).then_inc(s["hT_high_ready"], 1)

        def edge_coefficients(dve):
            dve.wait_ge(s["etype_in"], 16)
            dve.wait_ge(s["comp_in"], 32)
            dve.wait_ge(s["weight_in"], 16)
            nc.vector.tensor_copy(edge_f[:, 3, :], edge_i[:, 3, :]).then_inc(s["coef_steps"], 1)
            dve.wait_ge(s["coef_steps"], 1)
            nc.vector.tensor_tensor(is_type[:], edge_f[:, 3, :].unsqueeze(2).broadcast_to([P, EC, ET]),
                                    iota[:, 0:ET].unsqueeze(1).broadcast_to([P, EC, ET]), ALU.is_equal
                                    ).then_inc(s["coef_steps"], 1)
            dve.wait_ge(s["coef_steps"], 2)
            for layer in range(2):
                nc.vector.tensor_tensor(
                    typed[:], is_type[:].unsqueeze(2).broadcast_to([P, EC, EB, ET]),
                    comp[:, layer, :].rearrange("p (t b) -> p b t", t=ET).unsqueeze(1).broadcast_to([P, EC, EB, ET]),
                    ALU.mult).then_inc(s["coef_steps"], 1)
                dve.wait_ge(s["coef_steps"], 3 + 2 * layer)
                nc.vector.tensor_reduce(coef[:, :, layer, :], typed[:], X, ALU.add).then_inc(s["coef_steps"], 1)
                dve.wait_ge(s["coef_steps"], 4 + 2 * layer)
            both = coef[:].rearrange("p e l b -> p e (l b)")
            nc.vector.tensor_tensor(both, both, weight[:].unsqueeze(2).broadcast_to([P, EC, 2 * EB]), ALU.mult
                                    ).then_inc(s["coef_ready"], 1)

        def gat_softmax(dve, g):
            def step(ins, n):
                ins.then_inc(s["softmax_step"], 1)
                dve.wait_ge(s["softmax_step"], 7 * g + n)

            def per_head(ap):
                return ap.unsqueeze(2).broadcast_to([N, GH, N])

            def every_head(ap):
                return ap.unsqueeze(1).broadcast_to([N, GH, N])

            dve.wait_ge(s["e_done"], g + 1)
            step(nc.vector.tensor_tensor(score, bank[5][0:N, 0:GH * N].rearrange("p (g n) -> p g n", g=GH),
                                         per_head(al[:, 1, :]), ALU.add), 1)
            step(nc.vector.scalar_tensor_tensor(out=score2, in0=score, scalar=0.2, in1=score,
                                                op0=ALU.mult, op1=ALU.max), 2)
            step(nc.vector.tensor_tensor(score, score2, every_head(absent[:]), ALU.add), 3)
            step(nc.vector.tensor_reduce(stat[:, GAT_MAX:GAT_MAX + GH], score, X, ALU.max), 4)
            nc.vector.tensor_tensor(score, score, per_head(stat[:, GAT_MAX:GAT_MAX + GH]), ALU.subtract
                                    ).then_inc(s["s_masked"], 1)
            dve.wait_ge(s["s_exp"], g + 1)
            step(nc.vector.tensor_tensor(score2, score2, every_head(gat_count[:]), ALU.mult), 5)
            step(nc.vector.tensor_reduce(stat[:, GAT_SUM:GAT_SUM + GH], score2, X, ALU.add), 6)
            step(nc.vector.reciprocal(stat[:, GAT_RCP:GAT_RCP + GH], stat[:, GAT_SUM:GAT_SUM + GH]), 7)
            nc.vector.tensor_tensor(score2, score2, per_head(stat[:, GAT_RCP:GAT_RCP + GH]), ALU.mult
                                    ).then_inc(s["alpha_ready"], 1)

        def basis_tile(pe, layer, it, u):
            for half in range(HALVES):
                slot = HALVES * u + half
                pe.wait_ge(half_in[slot], it * 16 + (layer * TILES // LOOP_TILES + 1) * 16)
                for step in range(STEPS // HALVES):
                    q = half * (STEPS // HALVES) + step
                    for j in range(GROUPS):
                        c = (j * (STEPS // HALVES) + step) * D
                        mm = nc.tensor.matmul(bank[u % 2][32 * j:32 * j + 32, :],
                                              att_w[:, layer, q * 32:(q + 1) * 32], ring[0:BP, slot, c:c + D],
                                              start=(q == 0), stop=(q == STEPS - 1))
                mm.then_inc(s["half_free"], 1)
            mm_tile = it * LOOP_TILES + (layer * TILES + u + 1)
            pe.wait_ge(s["w_copied"], mm_tile)
            pe.wait_ge(s["y_ready"], mm_tile)
            nc.tensor.matmul(bank[2][0:N, :], y_now[:, u, :], w_sb[:, u % 2, :], start=False, stop=True,
                             skip_group_check=True).then_inc(s["contracted"], 1)

        def edge_mixes(pe):
            def chunk(c, b, start, stop):
                pe.wait_ge(s["hot_c_ready"], c + 1)
                pe.wait_ge(s["hot_w_ready"], c + 1)
                for n in range(2):
                    mm = nc.tensor.matmul(bank[6 + n][0:N, 0:EB * N], src_c[:, b, :],
                                          work[:, b, n * EB * N:(n + 1) * EB * N], start=start, stop=stop)
                mm.then_inc(s["hot_w_used"], 1)

            for b in range(2):
                chunk(b, b, b == 0, False)
            with pe.Fori(1, EC // 2 - 1) as it:
                for b in range(2):
                    chunk(it * 2 + b, b, False, False)
            for b in range(2):
                chunk(EC - 2 + b, b, False, b == 1)

        def gat_vectors(pe):
            for g in range(8):
                if g >= 2:
                    pe.wait_ge(s["avec_ready"], g - 1)
                nc.tensor.matmul(bank[4 + g % 2][0:N, :], pick(ROW_A + g), rows[:], start=True, stop=True
                                 ).then_inc(s["avec_done"], 1)
            pe.wait_ge(s["avec_ready"], 8)

        def gat_transposes(pe, g):
            def turn(source, first, to, done):
                for k in range(4):
                    c = (first + k) * P
                    mm = nc.tensor.transpose(to[:, k * N:(k + 1) * N], source[:, c:c + P], ident[0:N, 0:N])
                mm.then_inc(s[done], 1)

            if g == 0:
                pe.wait_ge(s["h_ready"], 4)
                turn(h, 0, bank[3], "hT_done")
            else:
                pe.wait_ge(s["gat_ready_a"], g)
                turn(gat_o, 0, bank[3], "hT_done")
                pe.wait_ge(s["gat_ready_b"], g)
                turn(gat_o, 4, bank[4], "hT_high_done")
            pe.wait_ge(s["hT_ready"], 4 + g)

        @block.sync
        def _(sp):
            sp.dma_start(x[:], io["x"]).then_inc(s["x_in"], 16)
            for n, w in enumerate((io["L0_gnn_Wq"], io["L0_gnn_Wk"])):
                sp.dma_start(wqk[:, n, :, :], chunked(w)[:, :, D - HD:D]).then_inc(s["wqk_in"], 16)
            sp.dma_start(wv, chunked(io["L0_gnn_Wv"])).then_inc(s["wv_in"], 16)
            for layer, basis in enumerate((io["L1_gnn_basis1"], io["L1_gnn_basis2"])):
                view = basis.rearrange("b (t k j h q) o -> t h b k j (q o)", t=TILES, k=BLOCKS, j=GROUPS, h=HALVES)
                with sp.Fori(0, TILES // LOOP_TILES) as it:
                    for slot in range(SLOTS):
                        sp.wait_ge(s["half_free"], it * SLOTS + (layer * TILES * HALVES + slot + 1))
                        tile = view[bass.ds(it * LOOP_TILES + slot // HALVES, 1), slot % HALVES]
                        sp.dma_start(ring[0:BP, slot, :].rearrange("p (j f) -> p j f", j=GROUPS),
                                     tile.rearrange("t b k j f -> (t b) k j f")).then_inc(half_in[slot], 16)

            def slot_free(slot):
                sp.wait_ge(s["half_free"], 2 * TILES * HALVES + slot + 1)

            w1, w2 = chunked(io["L2_gnn_W1"]), chunked(io["L2_gnn_W2"])
            slot_free(0)
            sp.dma_start(W1[:, :, 0:D], w1[:, :, 0:D]).then_inc(s["w1_in"], 16)
            sp.dma_start(W1[:, :, D:GD], w1[:, :, D:GD]).then_inc(s["w1b_in"], 16)
            slot_free(1)
            sp.dma_start(W2[:, 0:4, :], w2[:, 0:4, :]).then_inc(s["w2_in"], 16)
            slot_free(2)
            sp.dma_start(W2[:, 4:8, :], w2[:, 4:8, :]).then_inc(s["w2b_in"], 16)
            slot_free(3)
            sp.dma_start(Wfc, chunked(io["L2_gnn_Wfc"])).then_inc(s["wfc_in"], 16)

            def bases(to, basis, b):
                return sp.dma_start(to, basis[b:b + 2].rearrange("b (k p) f -> p (b k) f", p=P))

            slot_free(4)
            bases(ring[:, 4, :].rearrange("p (c f) -> p c f", c=8), io["L3_gnn_basis0"], 0).then_inc(s["b0a_in"], 16)
            slot_free(5)
            bases(ring[:, 5, :].rearrange("p (c f) -> p c f", c=8), io["L3_gnn_basis0"], 2).then_inc(s["b0b_in"], 16)
            slot_free(6)
            sp.dma_start(conv_w[0][4], chunked(io["L3_gnn_loop0"])).then_inc(s["loops_in"], 16)
            sp.dma_start(conv_w[1][4], chunked(io["L3_gnn_loop1"])).then_inc(s["loops_in"], 16)
            slot_free(7)
            bases(ring[:, 7, :].rearrange("p (c f) -> p c f", c=8), io["L3_gnn_basis1"], 0).then_inc(s["b1a_in"], 16)
            sp.wait_ge(s["proj_b"], 1)
            bases(ring[:, 0, :].rearrange("p (c f) -> p c f", c=8), io["L3_gnn_basis1"], 2).then_inc(s["b1b_in"], 16)

            sp.wait_ge(s["result_ready"], 1)
            sp.dma_start(out, x[:]).then_inc(s["out_done"], 16)
            sp.wait_ge(s["out_done"], 16)

        @block.gpsimd
        def _(pool):
            nc.gpsimd.memset(stat[0:1, 13:14], 0.0).then_inc(s["half_free"], SLOTS)
            nc.gpsimd.memset(stat[0:1, 14:15], 0.0).then_inc(s["contracted"], LOOP_TILES)
            nc.gpsimd.memset(stat[0:1, 15:16], 0.0).then_inc(s["hot_w_used"], 2)
            nc.gpsimd.iota(iota[:], [[1, N]], base=0, channel_multiplier=0,
                           allow_small_or_imprecise_dtypes=True).then_inc(s["iota_ready"], 1)
            nc.gpsimd.memset(ident[:], 0.0).then_inc(s["ident_ready"], 1)
            pool.wait_ge(s["ident_ready"], 1)
            nc.gpsimd.affine_select(out=ident[:], in_=ident[:], compare_op=ALU.not_equal, fill=1.0, base=0,
                                    pattern=[[-1, P]], channel_multiplier=1).then_inc(s["ident_ready"], 1)
            nc.gpsimd.memset(stat[:, NEG_HALF:NEG_HALF + 1], -0.5).then_inc(s["consts_ready"], 1)
            nc.gpsimd.memset(ones[:], 1.0).then_inc(s["consts_ready"], 1)
            nc.gpsimd.memset(uniform[:], 1.0 / N).then_inc(s["consts_ready"], 1)

            rstd_pow(pool, 1)

            nc.gpsimd.memset(mixed[:], 0.0).then_inc(s["mixed_zero"], 1)
            rstd_pow(pool, 2)

            pool.wait_ge(s["coef_ready"], 1)
            with pool.Fori(0, EC // 2) as it:
                for b in range(2):
                    pool.wait_ge(s["hot_w_used"], it * 2 + (b + 1))
                    nc.gpsimd.tensor_copy(src_c[:, b:b + 1, :], src_hot[:, bass.ds(it * 2 + b, 1), :]
                                          ).then_inc(s["hot_c_ready"], 1)
                    nc.gpsimd.tensor_tensor(
                        work[:, b, :].rearrange("p (c n) -> p c n", n=N),
                        dst_hot[:, bass.ds(it * 2 + b, 1), :].broadcast_to([P, 2 * EB, N]),
                        coef[:, bass.ds(it * 2 + b, 1), :, :].rearrange("p e l b -> p (e l b)").unsqueeze(2)
                        .broadcast_to([P, 2 * EB, N]),
                        ALU.mult).then_inc(s["hot_w_ready"], 1)
            rstd_pow(pool, 3)
            rstd_pow(pool, 4)

        @block.scalar
        def _(act):
            for n, name in enumerate(("src", "dst")):
                act.dma_start(edge_i[:, n, :], io[name].rearrange("(p c) -> p c", p=P)).then_inc(s["edges_in"], 16)
            act.dma_start(edge_i[:, 2, :], io["edge_type_2"].rearrange("(p c) -> p c", p=P)).then_inc(s["rel_in"], 16)

            def row(ap):
                return ap.rearrange("(a f) -> a f", a=1)

            act.dma_start(bqk[:, 0, :], row(io["L0_gnn_bq"])[:, D - HD:D]).then_inc(s["bqk_in"], 16)
            act.dma_start(bqk[:, 1, :], row(io["L0_gnn_bk"])[:, D - HD:D]).then_inc(s["bqk_in"], 16)
            act.dma_start(rows[ROW_BV:ROW_BV + 1, :], row(io["L0_gnn_bv"])).then_inc(s["bv_in"], 16)
            for layer in range(2):
                act.dma_start(att_rows[layer * NR:(layer + 1) * NR, :], io[f"L1_gnn_att{layer + 1}"]
                              ).then_inc(s["att_in"], 16)
                act.dma_start(gate_rows[layer * NR:(layer + 1) * NR, :],
                              io[f"L1_gnn_gate_w{layer + 1}"].rearrange("r f a -> r (f a)")).then_inc(s["gate_in"], 16)
            act.dma_start(root1, chunked(io["L1_gnn_root1"])).then_inc(s["root1_in"], 16)
            act.dma_start(edge_i[:, 3, :], io["edge_type_8"].rearrange("(p c) -> p c", p=P)).then_inc(s["etype_in"], 16)
            act.dma_start(weight[:], io["edge_weight"].rearrange("(p c) -> p c", p=P)).then_inc(s["weight_in"], 16)
            for layer in range(2):
                act.dma_start(comp[:, layer, :], io[f"L3_gnn_comp{layer}"].rearrange("t b -> (t b)").partition_broadcast(P)
                              ).then_inc(s["comp_in"], 16)
            single = ((ROW_L1B, "L1_gnn_bias1"), (ROW_L1B + 1, "L1_gnn_bias2"), (ROW_BFC, "L2_gnn_bfc"),
                      (ROW_L3B, "L3_gnn_bias0"), (ROW_L3B + 1, "L3_gnn_bias1"))
            double = ((ROW_B1, io["L2_gnn_b1"]), (ROW_B2, io["L2_gnn_b2"]))
            avecs = [io[f"L2_gnn_{n}"].rearrange("g c -> (g c)") for n in ("a_src1", "a_dst1", "a_src2", "a_dst2")]
            for r, name in single:
                act.dma_start(rows[r:r + 1, :], row(io[name])).then_inc(s["rows_in"], 16)
            for r, ap in double + tuple((ROW_A + 2 * n, a) for n, a in enumerate(avecs)):
                act.dma_start(rows[r:r + 2, :], ap.rearrange("(a f) -> a f", a=2)).then_inc(s["rows_in"], 16)
            act.dma_start(root2, chunked(io["L1_gnn_root2"])).then_inc(s["root2_in"], 16)

            act.wait_ge(s["qk_done"], 1)
            nc.scalar.copy(qk, bank[5][0:HD, 0:2 * N].rearrange("p (a n) -> p a n", a=2)).then_inc(s["qk_ready"], 1)
            act.wait_ge(s["v_done"], 1)
            nc.scalar.copy(v, bank[6][0:N, :]).then_inc(s["v_ready"], 1)
            act.wait_ge(s["max_ready"], 1)
            nc.scalar.activation(score[:, 1, :], score[:, 0, :], ACT.Exp, bias=stat[:, NEG_MAX:NEG_MAX + 1],
                                 accum_out=stat[:, EXP_SUM:EXP_SUM + 1]).then_inc(s["exp_ready"], 1)

            for layer in range(2):
                act.wait_ge(s["gates_done"], layer + 1)
                nc.scalar.activation(z_exp[:], bank[4][0:N, 0:NR], ACT.Exp, scale=-1.0).then_inc(s["z_ready"], 1)
                act.wait_ge(s["yT_done"], 2 * layer + 1)
                if layer:
                    act.wait_ge(s["y_ready"], TILES)
                nc.scalar.copy(yT[:, 0:4, :], bank[5][:, 0:4 * N].rearrange("p (t n) -> p t n", t=4)
                               ).then_inc(s["yT_a"], 1)
                with act.Fori(0, TILES // LOOP_TILES) as it:
                    for u in range(LOOP_TILES):
                        act.wait_ge(s["half_free"], it * SLOTS + (SLOTS + HALVES * (layer * TILES + u + 1)))
                        nc.scalar.copy(w_sb[:, u % 2, :], bank[u % 2][:]).then_inc(s["w_copied"], 1)
                if layer == 0:
                    for g in range(8):
                        act.wait_ge(s["avec_done"], g + 1)
                        nc.scalar.copy(avec[:, g // 2, (g % 2) * D:(g % 2 + 1) * D], bank[4 + g % 2][0:N, :]
                                       ).then_inc(s["avec_ready"], 1)

            for g in range(2):
                if g == 1:
                    copy_hT_high(act, 1)
                act.wait_ge(s["proj_a"], g + 1)
                nc.scalar.copy(gat_h[:, 0:D], bank[0][0:N, :]).then_inc(s["h_copied"], 1)
                act.wait_ge(s["proj_b"], g + 1)
                nc.scalar.copy(gat_h[:, D:GD], bank[1][0:N, :]).then_inc(s["h_copied"], 1)
                act.wait_ge(s["s_masked"], g + 1)
                nc.scalar.activation(score2, score, ACT.Exp).then_inc(s["s_exp"], 1)
                act.wait_ge(s["gat_out_b"], g + 1)
                nc.scalar.activation(gat_o[:, D:GD], bank[2][0:N, :], ACT.Relu).then_inc(s["gat_ready_b"], 1)
            copy_hT_high(act, 2)
            for layer in range(2):
                for k in (1, 3):
                    act.wait_ge(s["zT_done"], layer * KC + k + 1)
                    nc.scalar.copy(zT[:, k, :], bank[3 + k][:, 0:5 * N]).then_inc(s["zT_act"], 1)

        @block.vector
        def _(dve):
            def layer_norm(n):
                nc.vector.bn_stats(stat[:, BN:BN + 6], x[:]).then_inc(s["ln_stats"], 1)
                dve.wait_ge(s["ln_stats"], 2 * n - 1)
                nc.vector.bn_aggr(stat[:, MEAN:MEAN + 2], stat[:, BN:BN + 6]).then_inc(s["ln_stats"], 1)
                dve.wait_ge(s["ln_stats"], 2 * n)
                nc.vector.tensor_scalar(stat[:, VAR_EPS:VAR_EPS + 1], stat[:, VAR:VAR + 1], EPS, None, ALU.add
                                        ).then_inc(s["ln_var"], 1)
                dve.wait_ge(s["ln_rstd"], n)
                nc.vector.tensor_scalar(h[:], x[:], stat[:, MEAN:MEAN + 1], stat[:, RSTD:RSTD + 1], ALU.subtract, ALU.mult
                                        ).then_inc(s["ln_scaled"], 1)
                dve.wait_ge(s["ln_scaled"], n)
                nc.vector.tensor_scalar(h[:], h[:], 0.0, None, ALU.max).then_inc(s["h_ready"], 1)

            def copy_hT(n):
                dve.wait_ge(s["hT_done"], n)
                nc.vector.tensor_copy(hT[:, 0:4, :], bank[3][:, 0:4 * N].rearrange("p (k n) -> p k n", k=4)
                                      ).then_inc(s["hT_ready"], 1)

            dve.wait_ge(s["x_in"], 16)
            layer_norm(1)
            dve.wait_ge(s["edges_in"], 32)
            nc.vector.tensor_copy(edge_f[:, 0:2, :], edge_i[:, 0:2, :]).then_inc(s["edges_float"], 1)
            dve.wait_ge(s["rel_in"], 16)
            nc.vector.tensor_copy(edge_f[:, 2, :], edge_i[:, 2, :]).then_inc(s["edges_float"], 1)
            dve.wait_ge(s["edges_float"], 2)
            nc.vector.tensor_scalar(is_rel0[:], edge_f[:, 2, :], 0.0, None, ALU.is_equal).then_inc(s["edges_float"], 1)

            dve.wait_ge(s["iota_ready"], 1)
            every_node = iota[:].unsqueeze(1).broadcast_to([P, EC, N])
            for n, hot in enumerate((src_hot, dst_hot)):
                nc.vector.tensor_tensor(hot, edge_f[:, n, :].unsqueeze(2).broadcast_to([P, EC, N]), every_node,
                                        ALU.is_equal).then_inc(s["hots_ready"], 1)
            dve.wait_ge(s["edges_float"], 3)
            dve.wait_ge(s["hots_ready"], 2)
            nc.vector.tensor_tensor(src_hot0, src_hot, is_rel0[:].unsqueeze(2).broadcast_to([P, EC, N]),
                                    ALU.mult).then_inc(s["hot0_ready"], 1)
            dve.wait_ge(s["ident_ready"], 2)
            dve.wait_ge(s["att_in"], 32)
            nc.vector.tensor_copy(expand, att_rows[:].unsqueeze(2).broadcast_to([2 * NR, NB, BLOCKS])
                                  ).then_inc(s["expand_ready"], 1)
            nc.vector.tensor_reduce(same_block[:], ident[0:BP, 0:BP].rearrange("p (b k) -> p k b", k=BLOCKS), X, ALU.add
                                    ).then_inc(s["block_ready"], 1)
            nc.vector.memset(att_w[:], 0.0).then_inc(s["attw_zero"], 1)
            copy_hT(1)

            dve.wait_ge(s["counts_done"], 1)
            nc.vector.tensor_scalar(has_edge[:], bank[4][0:N, 0:N], 0.0, None, ALU.is_gt).then_inc(s["edge_mask"], 1)
            nc.vector.tensor_copy(relT[:, 0, :], bank[4][0:N, 2 * N:3 * N]).then_inc(s["rel_ready"], 1)
            nc.vector.tensor_tensor(gat_count[:], bank[4][0:N, N:2 * N], ident[0:N, 0:N], ALU.add
                                    ).then_inc(s["gat_mask"], 1)
            dve.wait_ge(s["rel_ready"], 1)
            nc.vector.tensor_tensor(relT[:, 1, :], bank[4][0:N, N:2 * N], relT[:, 0, :], ALU.subtract
                                    ).then_inc(s["rel_ready"], 1)
            dve.wait_ge(s["gat_mask"], 1)
            nc.vector.tensor_scalar(absent[:], gat_count[:], 0.0, ABSENT, ALU.is_equal, ALU.mult
                                    ).then_inc(s["gat_mask"], 1)

            dve.wait_ge(s["scores_done"], 1)
            dve.wait_ge(s["edge_mask"], 1)
            nc.vector.scalar_tensor_tensor(out=score[:, 0, :], in0=bank[7][0:N, 0:N], scalar=float(HD) ** -0.5,
                                           in1=has_edge[:], op0=ALU.mult, op1=ALU.mult).then_inc(s["masked"], 1)
            dve.wait_ge(s["masked"], 1)
            nc.vector.tensor_reduce(stat[:, NEG_MAX:NEG_MAX + 1], score[:, 0, :], X, ALU.max, negate=True
                                    ).then_inc(s["max_ready"], 1)
            dve.wait_ge(s["exp_ready"], 1)
            nc.vector.reciprocal(stat[:, EXP_RCP:EXP_RCP + 1], stat[:, EXP_SUM:EXP_SUM + 1]).then_inc(s["masked"], 1)
            dve.wait_ge(s["masked"], 2)
            nc.vector.tensor_scalar(score[:, 1, :], score[:, 1, :], stat[:, EXP_RCP:EXP_RCP + 1], None, ALU.mult
                                    ).then_inc(s["att_norm"], 1)
            dve.wait_ge(s["att_turned"], 1)
            nc.vector.tensor_copy(alphaT[:, 0, :], bank[3][0:N, 0:N]).then_inc(s["att_turned_ready"], 1)
            dve.wait_ge(s["attn_done"], 1)
            nc.vector.tensor_tensor(x[:], x[:], bank[5][0:N, :], ALU.add).then_inc(s["x_ready"], 1)
            dve.wait_ge(s["x_ready"], 1)
            layer_norm(2)

            dve.wait_ge(s["attp_done"], 1)
            nc.vector.tensor_copy(att_p[:], bank[7][0:BP, 0:2 * NR]).then_inc(s["attp_ready"], 1)
            dve.wait_ge(s["attp_ready"], 1)
            dve.wait_ge(s["block_ready"], 1)
            dve.wait_ge(s["attw_zero"], 1)
            for layer in range(2):
                for r in range(NR):
                    nc.vector.tensor_scalar(
                        att_w[:, layer, :].rearrange("p (q c) -> p q c", q=STEPS)[:, :, 4 * r:4 * r + 4],
                        same_block[:].unsqueeze(1).broadcast_to([BP, STEPS, BLOCKS]),
                        att_p[:, layer * NR + r:layer * NR + r + 1], None, ALU.mult).then_inc(s["attw_ready"], 1)
            dve.wait_ge(s["gateT_done"], 1)
            nc.vector.tensor_copy(gateT[:], bank[6][:, 0:KC * 2 * NR].rearrange("p (k g) -> p k g", k=KC)
                                  ).then_inc(s["gateT_ready"], 1)

            for layer in range(2):
                copy_hT(2 + layer)
                dve.wait_ge(s["z_ready"], layer + 1)
                nc.vector.tensor_scalar(gate[:], z_exp[:], 1.0, None, ALU.add).then_inc(s["gate_p1"], 1)
                dve.wait_ge(s["gate_p1"], layer + 1)
                nc.vector.reciprocal(gate[:], gate[:]).then_inc(s["gate_ready"], 1)
                dve.wait_ge(s["gate_ready"], layer + 1)
                dve.wait_ge(s["mixed_zero"], 1)
                for r in range(NR):
                    nc.vector.tensor_scalar(
                        mixed[:, r, :].rearrange("p (t s r k) -> p t s r k", t=TILES, r=NR, k=BLOCKS)[:, :, :, r, :],
                        h[:].rearrange("p (t k s) -> p t s k", t=TILES, k=BLOCKS),
                        gate[:, r:r + 1], None, ALU.mult).then_inc(s["mixed_ready"], 1)
                dve.wait_ge(s["yT_done"], 2 * layer + 2)
                nc.vector.tensor_copy(yT[:, 4:8, :], bank[6][:, 0:4 * N].rearrange("p (t n) -> p t n", t=4)
                                      ).then_inc(s["yT_ready"], 1)
                if layer == 0:
                    edge_coefficients(dve)
                dve.wait_ge(s["yT_a"], layer + 1)
                dve.wait_ge(s["yT_ready"], layer + 1)
                with dve.Fori(0, TILES // LOOP_TILES) as it:
                    for u in range(LOOP_TILES):
                        dve.wait_ge(s["contracted"], it * LOOP_TILES + (layer * TILES + u + 1))
                        nc.vector.tensor_copy(y_now[:, u:u + 1, :], yT[:, bass.ds(it * LOOP_TILES + u, 1), :]
                                              ).then_inc(s["y_ready"], 1)
                dve.wait_ge(s["contracted"], LOOP_TILES + (layer + 1) * TILES)
                if layer == 0:
                    nc.vector.tensor_scalar(h[:], bank[2][0:N, :], 0.0, None, ALU.max).then_inc(s["h_ready"], 1)
                    for n in range(2):
                        dve.wait_ge(s["hot_w_used"], 2 + EC)
                        nc.vector.tensor_copy(mix3[:, n, 0:EB * N], bank[6 + n][0:N, 0:EB * N]).then_inc(s["mix_ready"], 1)
                        nc.vector.tensor_copy(mix3[:, n, EB * N:], ident[0:N, 0:N]).then_inc(s["mix_ready"], 1)
                else:
                    nc.vector.tensor_tensor(x[:], x[:], bank[2][0:N, :], ALU.add).then_inc(s["x_ready"], 1)
                    dve.wait_ge(s["x_ready"], 2)
                    layer_norm(3)

            for g in range(2):
                copy_hT(4 + g)
                for half in range(2):
                    dve.wait_ge(s["h_copied"], 2 * g + half + 1)
                    dve.wait_ge(s["avec_ready"], 8)
                    for head in (2 * half, 2 * half + 1):
                        for n in range(2):
                            cols = slice(head * GC, (head + 1) * GC)
                            dot = 2 * head + n
                            if dot >= len(dot_out):
                                dve.wait_ge(s["al_ready"], 8 * g + dot - len(dot_out) + 1)
                            nc.vector.tensor_tensor_reduce(
                                out=dot_out[dot % len(dot_out)], in0=gat_h[:, cols], in1=avec[:, 2 * g + n, cols], scale=1.0, scalar=0.0,
                                op0=ALU.mult, op1=ALU.add, accum_out=al[:, n, head:head + 1]).then_inc(s["al_ready"], 1)
                dve.wait_ge(s["al_ready"], 8 * (g + 1))
                nc.vector.tensor_tensor(score, ident[0:N, 0:N].unsqueeze(1).broadcast_to([N, GH, N]),
                                        al[:, 0, :].unsqueeze(2).broadcast_to([N, GH, N]), ALU.mult
                                        ).then_inc(s["diag_ready"], 1)
                gat_softmax(dve, g)
                dve.wait_ge(s["alpha_done"], g + 1)
                nc.vector.tensor_copy(alphaT, bank[6][0:N, 0:GH * N].rearrange("p (g n) -> p g n", g=GH)
                                      ).then_inc(s["alphaT_ready"], 1)
                dve.wait_ge(s["gat_out_a"], g + 1)
                nc.vector.tensor_scalar(gat_o[:, 0:D], bank[7][0:N, :], 0.0, None, ALU.max).then_inc(s["gat_ready_a"], 1)

            copy_hT(6)
            dve.wait_ge(s["fc_done"], 1)
            nc.vector.tensor_tensor(x[:], x[:], bank[0][0:N, :], ALU.add).then_inc(s["x_ready"], 1)
            dve.wait_ge(s["x_ready"], 3)
            layer_norm(4)
            for layer in range(2):
                for k in (0, 2):
                    dve.wait_ge(s["zT_done"], layer * KC + k + 1)
                    nc.vector.tensor_copy(zT[:, k, :], bank[3 + k][:, 0:5 * N]).then_inc(s["zT_dve"], 1)
                dve.wait_ge(s["conv_done"], layer + 1)
                if layer == 0:
                    nc.vector.tensor_scalar(h[:], bank[7][0:N, :], 0.0, None, ALU.max).then_inc(s["h_ready"], 1)
                else:
                    nc.vector.tensor_tensor(x[:], x[:], bank[2][0:N, :], ALU.add).then_inc(s["result_ready"], 1)

        @block.tensor
        def _(pe):
            def transposes(source, n, to, done):
                for k in range(4):
                    c = (n + k) * P
                    mm = nc.tensor.transpose(to[:, k * N:(k + 1) * N], source[:, c:c + P], ident[0:N, 0:N])
                mm.then_inc(s[done], 1)

            pe.wait_ge(s["ident_ready"], 2)
            pe.wait_ge(s["h_ready"], 1)
            transposes(h, 0, bank[3], "hT_done")
            pe.wait_ge(s["hT_ready"], 1)
            pe.wait_ge(s["wqk_in"], 32)
            pe.wait_ge(s["bqk_in"], 32)
            pe.wait_ge(s["consts_ready"], 3)
            for n in range(2):
                q_ps = bank[5][0:HD, n * N:(n + 1) * N]
                nc.tensor.matmul(q_ps, bqk[:, n, :], ones[0:1, :], start=True, stop=False)
                for k in range(KC):
                    mm = nc.tensor.matmul(q_ps, wqk[:, n, k, :], hT[:, k, :], start=False, stop=(k == KC - 1))
            mm.then_inc(s["qk_done"], 1)
            pe.wait_ge(s["hots_ready"], 2)
            pe.wait_ge(s["hot0_ready"], 1)
            for n, (left, right) in enumerate(((src_hot, dst_hot), (dst_hot, src_hot), (dst_hot, src_hot0))):
                for c in range(EC):
                    mm = nc.tensor.matmul(bank[4][0:N, n * N:(n + 1) * N], left[:, c, :], right[:, c, :],
                                          start=(c == 0), stop=(c == EC - 1))
            mm.then_inc(s["counts_done"], 1)
            pe.wait_ge(s["qk_ready"], 1)
            nc.tensor.matmul(bank[7][0:N, 0:N], qk[:, 0, :], qk[:, 1, :], start=True, stop=True).then_inc(s["scores_done"], 1)
            pe.wait_ge(s["bv_in"], 16)
            nc.tensor.matmul(bank[6][0:N, :], ones[0:1, :], rows[0:1, :], start=True, stop=False)
            pe.wait_ge(s["wv_in"], 16)
            for k in range(KC):
                mm = nc.tensor.matmul(bank[6][0:N, :], hT[:, k, :], wv[:, k, :], start=False, stop=(k == KC - 1))
            mm.then_inc(s["v_done"], 1)
            pe.wait_ge(s["v_ready"], 1)
            pe.wait_ge(s["gate_in"], 32)
            for k in range(KC):
                mm = nc.tensor.transpose(bank[6][:, k * 2 * NR:(k + 1) * 2 * NR], gate_rows[:, k * P:(k + 1) * P],
                                         ident[0:2 * NR, 0:2 * NR])
            mm.then_inc(s["gateT_done"], 1)
            pe.wait_ge(s["att_norm"], 1)
            nc.tensor.transpose(bank[3][0:N, 0:N], score[:, 1, :], ident[0:N, 0:N]).then_inc(s["att_turned"], 1)
            pe.wait_ge(s["expand_ready"], 1)
            nc.tensor.transpose(bank[7][0:BP, 0:2 * NR], expand.rearrange("p b k -> p (b k)"),
                                ident[0:2 * NR, 0:2 * NR]).then_inc(s["attp_done"], 1)
            pe.wait_ge(s["att_turned_ready"], 1)
            nc.tensor.matmul(bank[5][0:N, 0:D - HD], uniform[:], v[:, 0:D - HD], start=True, stop=True)
            nc.tensor.matmul(bank[5][0:N, D - HD:D], alphaT[:, 0, :], v[:, D - HD:D], start=True, stop=True
                             ).then_inc(s["attn_done"], 1)

            for layer in range(2):
                if layer:
                    edge_mixes(pe)
                    gat_vectors(pe)
                pe.wait_ge(s["h_ready"], 2 + layer)
                transposes(h, 0, bank[3], "hT_done")
                pe.wait_ge(s["hT_ready"], 2 + layer)
                pe.wait_ge(s["gateT_ready"], 1)
                pe.wait_ge(s["gat_mask"], 2)
                for k in range(KC):
                    mm = nc.tensor.matmul(bank[4][0:N, 0:NR], hT[:, k, :], gateT[:, k, layer * NR:(layer + 1) * NR],
                                          start=(k == 0), stop=(k == KC - 1))
                mm.then_inc(s["gates_done"], 1)
                pe.wait_ge(s["rows_in"], 16 * 11)
                nc.tensor.matmul(bank[2][0:N, :], pick(ROW_L1B + layer), rows[:], start=True, stop=True,
                                 skip_group_check=True)
                pe.wait_ge(s[f"root{layer + 1}_in"], 16)
                root = (root1, root2)[layer]
                for k in range(KC):
                    nc.tensor.matmul(bank[2][0:N, :], hT[:, k, :], root[:, k, :], start=False, stop=True,
                                     skip_group_check=True)
                pe.wait_ge(s["mixed_ready"], 2 * (layer + 1))
                pe.wait_ge(s["rel_ready"], 2)
                for t in range(TILES):
                    y_ps = bank[5 + t // 4][:, (t % 4) * N:(t % 4 + 1) * N]
                    for r in range(NR):
                        mm = nc.tensor.matmul(y_ps, mixed[:, r, t * P:(t + 1) * P], relT[:, r, :],
                                              start=(r == 0), stop=(r == NR - 1))
                    if t % 4 == 3:
                        mm.then_inc(s["yT_done"], 1)
                pe.wait_ge(s["attw_ready"], 4)
                with pe.Fori(0, TILES // LOOP_TILES) as it:
                    for u in range(LOOP_TILES):
                        basis_tile(pe, layer, it, u)

            for g in range(2):
                chunks = 4 * (g + 1)
                gat_transposes(pe, g)
                W = (W1, W2)[g]
                for half in range(2):
                    if half == 0:
                        pe.wait_ge(s[("w1_in", "w2_in")[g]], 16)
                    for k in range(chunks):
                        if k == 4 and half == 0:
                            pe.wait_ge(s["hT_high_ready"], 1)
                            pe.wait_ge(s["w2b_in"], 16)
                        if k == 0 and half == 1 and g == 0:
                            pe.wait_ge(s["w1b_in"], 16)
                        mm = nc.tensor.matmul(bank[half][0:N, :], hT[:, k, :], W[:, k, half * D:(half + 1) * D],
                                              start=(k == 0), stop=(k == chunks - 1))
                    mm.then_inc(s[("proj_a", "proj_b")[half]], 1)
                for half, ps in enumerate((bank[7], bank[2])):
                    nc.tensor.matmul(ps[0:N, :], pick((ROW_B1, ROW_B2)[g] + half), rows[:], start=True, stop=False)
                pe.wait_ge(s["diag_ready"], g + 1)
                nc.tensor.matmul(bank[5][0:N, 0:GH * N], ones[:], score.rearrange("p g n -> p (g n)"),
                                 start=True, stop=True).then_inc(s["e_done"], 1)
                pe.wait_ge(s["alpha_ready"], g + 1)
                for head in range(GH):
                    mm = nc.tensor.transpose(bank[6][0:N, head * N:(head + 1) * N], score2[:, head, :], ident[0:N, 0:N])
                mm.then_inc(s["alpha_done"], 1)
                pe.wait_ge(s["alphaT_ready"], g + 1)
                for head in range(GH):
                    ps = (bank[7], bank[2])[head // 2]
                    c = head % 2 * GC
                    mm = nc.tensor.matmul(ps[0:N, c:c + GC], alphaT[:, head, :], gat_h[:, head * GC:(head + 1) * GC],
                                          start=False, stop=(head % 2 == 1))
                    if head % 2:
                        mm.then_inc(s[("gat_out_a", "gat_out_b")[head // 2]], 1)

            gat_transposes(pe, 2)
            nc.tensor.matmul(bank[0][0:N, :], pick(ROW_BFC), rows[:], start=True, stop=False)
            pe.wait_ge(s["wfc_in"], 16)
            for k in range(8):
                if k == 4:
                    pe.wait_ge(s["hT_high_ready"], 2)
                mm = nc.tensor.matmul(bank[0][0:N, :], hT[:, k, :], Wfc[:, k, :], start=False, stop=(k == 7))
            mm.then_inc(s["fc_done"], 1)

            for layer in range(2):
                ps = (bank[7], bank[2])[layer]
                nc.tensor.matmul(ps[0:N, :], pick(ROW_L3B + layer), rows[:], start=True, stop=False)
                pe.wait_ge(s["h_ready"], 5 + layer)
                pe.wait_ge(s["mix_ready"], 4)
                for k in range(KC):
                    nc.tensor.matmul(bank[3 + k][:, 0:5 * N], h[:, k * P:(k + 1) * P], mix3[:, layer, :],
                                     start=True, stop=True).then_inc(s["zT_done"], 1)
                for name in (("b0a_in", "b0b_in"), ("b1a_in", "b1b_in"))[layer]:
                    pe.wait_ge(s[name], 16)
                pe.wait_ge(s["loops_in"], 32)
                for k in range(KC):
                    pe.wait_ge(s[("zT_dve", "zT_act")[k % 2]], 2 * layer + k // 2 + 1)
                    for b in range(EB + 1):
                        mm = nc.tensor.matmul(ps[0:N, :], zT[:, k, b * N:(b + 1) * N], conv_w[layer][b][:, k, :],
                                              start=False, stop=(k == KC - 1 and b == EB))
                mm.then_inc(s["conv_done"], 1)


_OUTS = [((N, D), "float32")]


def kernel(**inputs):
    import numpy as _np
    import concourse.bacc as _bacc
    from concourse import mybir as _mybir
    from concourse.bass_utils import run_bass_kernel_spmd as _run

    nc = _bacc.Bacc("TRN2", target_bir_lowering=False, num_devices=1)
    arrays, io = {}, {}
    for name in inputs:
        a = _np.ascontiguousarray(inputs[name])
        arrays[f"in_{name}_dram"] = a
        io[name] = nc.dram_tensor(f"in_{name}_dram", a.shape, _mybir.dt.from_np(a.dtype), kind="ExternalInput").ap()
    shape, dtype = _OUTS[0]
    result = nc.dram_tensor("out_0_dram", shape, _mybir.dt.from_np(_np.dtype(dtype)), kind="ExternalOutput").ap()
    gnn_blocks(nc, io, result)
    r = _run(nc, [arrays], core_ids=[0])
    return r.results[0]["out_0_dram"]
```

```python
from contextlib import ExitStack

import concourse.bass as bass
from concourse import mybir

F32 = mybir.dt.float32
BF16 = mybir.dt.bfloat16
I32 = mybir.dt.int32
ALU = mybir.AluOpType
ACT = mybir.ActivationFunctionType
X = mybir.AxisListType.X

N = 96
D = 512
E = 1536
P = 128
EC = E // P
KC = D // P
HEADS, HD = 8, 64
NB, NR = 30, 2
BLOCKS = 4
BP = NB * BLOCKS
GROUPS, STEPS = 4, 4
TILE = BLOCKS * GROUPS * STEPS
TILES = D // TILE
HALVES = 2
SLOTS = 8
LOOP_TILES = SLOTS // HALVES
GH, GC = 4, 256
GD = GH * GC
ET, EB = 8, 4
EPS = 1e-5
ABSENT = -1e30

ROW_BV, ROW_L1B, ROW_B1, ROW_B2, ROW_BFC, ROW_L3B = 0, 1, 3, 5, 7, 8
ROWS = 10


def gnn_blocks(nc, io, out):
    with ExitStack() as ctx:
        def sb(name, shape, dt=F32):
            return ctx.enter_context(nc.sbuf_tensor(name, shape, dt))

        def sem(name):
            return ctx.enter_context(nc.semaphore(name))

        ring = sb("ring", [P, SLOTS, 8 * D])
        early = sb("early", [P, 8 * D])
        wv = early[:, 0:4 * D].rearrange("p (k f) -> p k f", k=KC)
        root1 = early[:, 4 * D:8 * D].rearrange("p (k f) -> p k f", k=KC)
        avec = early[0:N, :].rearrange("p (g f) -> p g f", g=4)
        late = sb("late", [P, KC * 5 * N + 128])
        root2 = late[:, 0:4 * D].rearrange("p (k f) -> p k f", k=KC)
        bvec = late[0:N, :].rearrange("p (g f) -> p g f", g=2)
        zT = late[:, 0:KC * 5 * N].rearrange("p (k f) -> p k f", k=KC)
        wqk = sb("wqk", [P, 2, KC, HD])
        mixed = sb("mixed", [N, NR, TILES * P])
        gat_h = mixed[:, 0, :]
        gat_o = mixed[:, 1, :]
        yT = sb("yT", [P, TILES, N])
        y_now = sb("y_now", [P, LOOP_TILES, N])
        w_sb = sb("w_sb", [P, 2, D])
        x = sb("x", [N, D])
        h = sb("h", [N, D])
        hT = sb("hT", [P, 8, N])
        v = yT[0:N].rearrange("p t n -> p (t n)")[:, 0:D]
        qk = y_now[0:HD, 0:2, :]
        ident = sb("ident", [P, P])
        iota = sb("iota", [P, N])
        ones = sb("ones", [N, N])
        uniform = sb("uniform", [N, N])
        rows = sb("rows", [ROWS, D])
        bqk = sb("bqk", [1, 2, HD])
        gate_rows = sb("gate_rows", [2 * NR, D])
        gateT = sb("gateT", [P, KC, 2 * NR])
        edge_i = sb("edge_i", [P, 4, EC], I32)
        edge_f = sb("edge_f", [P, 4, EC])
        weight = sb("weight", [P, EC])
        comp = sb("comp", [P, 2, ET * EB])
        att_rows = sb("att_rows", [2 * NR, NB])
        att_p = sb("att_p", [BP, 2 * NR])
        same_block = sb("same_block", [BP, BLOCKS])
        att_w = sb("att_w", [BP, 2, 160])
        edge_area = sb("edge_area", [P, 3 * EC * N // 2])
        hots = edge_area[:].bitcast(BF16).rearrange("p (a e n) -> p a e n", a=3, e=EC)
        src_hot, dst_hot, src_hot0 = hots[:, 0], hots[:, 1], hots[:, 2]
        src_c = sb("src_c", [P, 2, N])
        mix3 = sb("mix3", [N, 2, 5 * N])
        is_rel0 = sb("is_rel0", [P, EC])
        has_edge = sb("has_edge", [N, N])
        relT = sb("relT", [N, NR, N])
        gat_count = sb("gat_count", [N, N])
        absent = sb("absent", [N, N])
        is_type = sb("is_type", [P, EC, ET])
        typed = sb("typed", [P, EC, EB, ET])
        coef = sb("coef", [P, EC, 2, EB])
        work = sb("work", [P, 2, 2 * EB * N])
        score = work[0:N, 0, 0:GH * N].rearrange("p (g s) -> p g s", g=GH)
        score2 = work[0:N, 0, GH * N:2 * GH * N].rearrange("p (g s) -> p g s", g=GH)
        alphaT = work[0:N, 1, 0:GH * N].rearrange("p (g s) -> p g s", g=GH)
        dot_out = [work[0:N, 1, GH * N:GH * N + GC], typed[0:N].rearrange("p e b t -> p (e b t)")[:, 0:GC]]
        expand = work[0:2 * NR, 1, GH * N + GC:GH * N + GC + BP].rearrange("p (b k) -> p b k", b=NB)
        avec_rows = work[0:LOOP_TILES].rearrange("p a f -> p (a f)")[:, 2 * N:16 * N].rearrange(
            "p (i f) -> p i f", i=2)[:, :, 0:D]
        al = sb("al", [N, 2, GH])
        stat = sb("stat", [N, 32])
        z_exp = sb("z_exp", [N, NR])
        gate = sb("gate", [N, NR])
        bank = [ctx.enter_context(nc.psum_tensor(f"bank{i}", [P, D], F32)) for i in range(8)]

        W1 = ring[:, 0, :].rearrange("p (k f) -> p k f", k=4)
        W2 = ring[:, 1:3, :].rearrange("p s (k f) -> p (s k) f", k=4)
        Wfc = ring[:, 3, :].rearrange("p (k f) -> p k f", k=8)
        conv_w = [[ring[:, slot, c * 4 * D:(c + 1) * 4 * D].rearrange("p (k f) -> p k f", k=KC) for slot, c in at]
                  for at in (((4, 0), (4, 1), (5, 0), (5, 1), (6, 0)), ((7, 0), (7, 1), (0, 0), (0, 1), (6, 1)))]

        names = """x_in edges_in rel_in wqk_in wv_in bias_in bqk_in rows_in avec_in gate_in att_in etype_in weight_in comp_in
            root1_in root2_in w1_in w1b_in w2_in w2b_in wfc_in b0a_in b0b_in loops_in b1a_in b1b_in out_done
            ident_ready iota_ready consts_ready edges_float hots_ready hot0_ready
            half_free w_copied y_ready contracted
            counts_done rel_ready edge_mask gat_mask
            ln_stats ln_var ln_rstd ln_centred h_ready hT_done hT_ready low_done low_ready high_done high_ready
            qk_done qk_ready v_done v_ready scores_done masked max_ready exp_ready att_norm att_turned att_turned_ready
            attn_done x_ready
            expand_ready attp_done attp_ready block_ready attw_zero attw_ready gateT_done gateT_ready
            gates_done z_ready gate_p1 gate_ready mixed_zero mixed_ready yT_done yT_a yT_ready agg_started
            coef_steps coef_ready hot_c_ready hot_w_ready hot_w_used mix_ready
            avec_done avec_ready
            bvec_done bvec_ready proj_done src_dots dst_dots diag_ready e_done softmax_step s_masked s_exp
            gat_h_ready alpha_ready alpha_sum gat_rcp alpha_turned alphaT_ready
            gat_out gat_low_ready gat_h2_ready gat_h3_ready
            fc_done zT_done zT_dve zT_act conv_done result_ready""".split()
        s = {n: sem(n) for n in names}
        half_in = [sem(f"half_in{i}") for i in range(SLOTS)]

        block = ctx.enter_context(nc.Block())

        def row(ap):
            return ap.rearrange("(a f) -> a f", a=1)

        def chunked(w):
            return w.rearrange("(k p) f -> p k f", p=P)

        BN, MEAN, VAR, VAR_EPS, RSTD, NEG_MAX, EXP_SUM, EXP_RCP, NEG_HALF = 0, 6, 7, 10, 11, 8, 9, 12, 16
        GAT_MAX, GAT_SUM, GAT_RCP = 20, 24, 28

        def pick(r, of=ROWS):
            return ident[0:of, r:r + 1].broadcast_to([of, N])

        def rstd_pow(pool, n):
            pool.wait_ge(s["consts_ready"], 1)
            pool.wait_ge(s["ln_var"], n)
            nc.gpsimd.tensor_tensor(stat[:, RSTD:RSTD + 1], stat[:, VAR_EPS:VAR_EPS + 1],
                                    stat[:, NEG_HALF:NEG_HALF + 1], ALU.pow).then_inc(s["ln_rstd"], 1)

        def copy_low(act, g):
            act.wait_ge(s["low_done"], g + 1)
            nc.scalar.copy(hT[:, 0:4, :], bank[3][:, 0:4 * N].rearrange("p (k n) -> p k n", k=4)
                           ).then_inc(s["low_ready"], 1)

        def evacuate(engine, head):
            to = gat_o[:, head * GC:(head + 1) * GC]
            ps = (bank[4], bank[4], bank[4], bank[5])[head][0:N, head % 2 * GC:(head % 2 + 1) * GC]
            scale = stat[:, GAT_RCP + head:GAT_RCP + head + 1]
            if engine is nc.scalar:
                return engine.activation(to, ps, ACT.Relu, scale=scale)
            return engine.tensor_scalar(to, ps, scale, 0.0, ALU.mult, ALU.max)

        def edge_coefficients(dve):
            dve.wait_ge(s["etype_in"], 16)
            dve.wait_ge(s["comp_in"], 32)
            dve.wait_ge(s["weight_in"], 16)
            nc.vector.tensor_copy(edge_f[:, 3, :], edge_i[:, 3, :]).then_inc(s["coef_steps"], 1)
            dve.wait_ge(s["coef_steps"], 1)
            nc.vector.tensor_tensor(is_type[:], edge_f[:, 3, :].unsqueeze(2).broadcast_to([P, EC, ET]),
                                    iota[:, 0:ET].unsqueeze(1).broadcast_to([P, EC, ET]), ALU.is_equal
                                    ).then_inc(s["coef_steps"], 1)
            dve.wait_ge(s["coef_steps"], 2)
            for layer in range(2):
                nc.vector.tensor_tensor(
                    typed[:], is_type[:].unsqueeze(2).broadcast_to([P, EC, EB, ET]),
                    comp[:, layer, :].rearrange("p (t b) -> p b t", t=ET).unsqueeze(1).broadcast_to([P, EC, EB, ET]),
                    ALU.mult).then_inc(s["coef_steps"], 1)
                dve.wait_ge(s["coef_steps"], 3 + 2 * layer)
                nc.vector.tensor_reduce(coef[:, :, layer, :], typed[:], X, ALU.add).then_inc(s["coef_steps"], 1)
                dve.wait_ge(s["coef_steps"], 4 + 2 * layer)
            both = coef[:].rearrange("p e l b -> p e (l b)")
            nc.vector.tensor_tensor(both, both, weight[:].unsqueeze(2).broadcast_to([P, EC, 2 * EB]), ALU.mult
                                    ).then_inc(s["coef_ready"], 1)

        def gat_softmax(dve, g, half):
            n = 2 * g + half + 1
            heads = slice(2 * half, 2 * half + 2)
            sc, sc2 = score[:, heads, :], score2[:, heads, :]

            def step(ins, k):
                ins.then_inc(s["softmax_step"], 1)
                dve.wait_ge(s["softmax_step"], 4 * (n - 1) + k)

            def per_head(ap):
                return ap.unsqueeze(2).broadcast_to([N, 2, N])

            def every_head(ap):
                return ap.unsqueeze(1).broadcast_to([N, 2, N])

            def dots(side, done):
                for head in (2 * half, 2 * half + 1):
                    nc.vector.tensor_tensor_reduce(
                        out=dot_out[head % 2], in0=gat_bank(g, half)[0:N, head % 2 * GC:(head % 2 + 1) * GC],
                        in1=avec[:, 2 * g + side, head * GC:(head + 1) * GC], scale=1.0, scalar=0.0,
                        op0=ALU.mult, op1=ALU.add, accum_out=al[:, side, head:head + 1]).then_inc(s[done], 1)

            def sum_up(m):
                pair = slice(2 * ((m - 1) % 2), 2 * ((m - 1) % 2) + 2)
                cols = slice(pair.start, pair.stop)
                dve.wait_ge(s["alpha_ready"], m)
                nc.vector.tensor_reduce(stat[:, GAT_SUM + cols.start:GAT_SUM + cols.stop], score2[:, pair, :], X, ALU.add
                                        ).then_inc(s["alpha_sum"], 1)
                dve.wait_ge(s["alpha_sum"], m)
                nc.vector.reciprocal(stat[:, GAT_RCP + cols.start:GAT_RCP + cols.stop],
                                     stat[:, GAT_SUM + cols.start:GAT_SUM + cols.stop]).then_inc(s["gat_rcp"], 1)

            dve.wait_ge(s["avec_ready"], 8)
            dve.wait_ge(s["bvec_ready"], 4)
            dve.wait_ge(s["proj_done"], n)
            if n > 1:
                dve.wait_ge(s["dst_dots"], 2 * (n - 1))
            dots(0, "src_dots")
            dve.wait_ge(s["src_dots"], 2 * n)
            nc.vector.tensor_tensor(sc, every_head(ident[0:N, 0:N]), per_head(al[:, 0, heads]), ALU.mult
                                    ).then_inc(s["diag_ready"], 1)
            dots(1, "dst_dots")
            if half:
                sum_up(n - 1)
            dve.wait_ge(s["dst_dots"], 2 * n)
            dve.wait_ge(s["e_done"], n)
            step(nc.vector.tensor_tensor(sc, bank[5][0:N, 2 * half * N:(2 * half + 2) * N].rearrange("p (g n) -> p g n", g=2),
                                         per_head(al[:, 1, heads]), ALU.add), 1)
            step(nc.vector.scalar_tensor_tensor(out=sc2, in0=sc, scalar=0.2, in1=sc, op0=ALU.mult, op1=ALU.max), 2)
            step(nc.vector.tensor_tensor(sc, sc2, every_head(absent[:]), ALU.add), 3)
            gat_max = stat[:, GAT_MAX + heads.start:GAT_MAX + heads.stop]
            step(nc.vector.tensor_reduce(gat_max, sc, X, ALU.max), 4)
            nc.vector.tensor_tensor(sc, sc, per_head(gat_max), ALU.subtract).then_inc(s["s_masked"], 1)
            cols = slice(half * D, (half + 1) * D)
            nc.vector.tensor_tensor(gat_h[:, cols], gat_bank(g, half)[0:N, :], bvec[:, g, cols], ALU.add
                                    ).then_inc(s["gat_h_ready"], 1)
            dve.wait_ge(s["s_exp"], n)
            nc.vector.tensor_tensor(sc2, sc2, every_head(gat_count[:]), ALU.mult).then_inc(s["alpha_ready"], 1)
            if half:
                sum_up(n)

        def gat_bank(g, half):
            return bank[((0, 1), (7, 2))[g][half]]

        def basis_product(pe, layer, it, u, half):
            slot = HALVES * u + half
            pe.wait_ge(half_in[slot], it * 16 + (layer * TILES // LOOP_TILES + 1) * 16)
            for step in range(STEPS // HALVES):
                q = half * (STEPS // HALVES) + step
                for j in range(GROUPS):
                    c = (j * (STEPS // HALVES) + step) * D
                    mm = nc.tensor.matmul(bank[u % 2][32 * j:32 * j + 32, :],
                                          att_w[:, layer, q * 32:(q + 1) * 32], ring[0:BP, slot, c:c + D],
                                          start=(q == 0), stop=(q == STEPS - 1))
            mm.then_inc(s["half_free"], 1)

        def contract(pe, layer, it, u):
            mm_tile = it * LOOP_TILES + (layer * TILES + u + 1)
            pe.wait_ge(s["w_copied"], mm_tile)
            pe.wait_ge(s["y_ready"], mm_tile)
            nc.tensor.matmul(bank[2][0:N, :], y_now[:, u, :], w_sb[:, u % 2, :], start=False, stop=True,
                             skip_group_check=True).then_inc(s["contracted"], 1)

        def open_edge_mixes(pe):
            pe.wait_ge(s["yT_ready"], 2)
            for n in range(2):
                nc.tensor.matmul(bank[6 + n][0:N, 0:EB * N], ident[0:1, 1:N + 1],
                                 ones[0:1, :].unsqueeze(1).broadcast_to([1, EB, N]), start=True, stop=True,
                                 skip_group_check=True)

        def edge_mix(pe, c, b):
            pe.wait_ge(s["hot_c_ready"], c + 1)
            pe.wait_ge(s["hot_w_ready"], c + 1)
            for n in range(2):
                mm = nc.tensor.matmul(bank[6 + n][0:N, 0:EB * N], src_c[:, b, :],
                                      work[:, b, n * EB * N:(n + 1) * EB * N], start=False, stop=True,
                                      skip_group_check=True)
            mm.then_inc(s["hot_w_used"], 1)

        def gat_vector(pe, it, u):
            nc.tensor.matmul(bank[3 + u % 2][0:N, :],
                             pick(u, LOOP_TILES), avec_rows[:, bass.ds(it, 1), :], start=True, stop=True).then_inc(s["avec_done"], 1)

        def bias_bank(g):
            return bank[(4, 3, 4, 5)[g]]

        def gat_biases(pe, gs):
            for g in gs:
                if g >= 2:
                    pe.wait_ge(s["bvec_ready"], g - 1)
                nc.tensor.matmul(bias_bank(g)[0:N, :], pick(ROW_B1 + g), rows[:], start=True, stop=True
                                 ).then_inc(s["bvec_done"], 1)

        def biases_out(act, gs):
            for g in gs:
                act.wait_ge(s["bvec_done"], g + 1)
                nc.scalar.copy(bvec[:, g // 2, (g % 2) * D:(g % 2 + 1) * D], bias_bank(g)[0:N, :]
                               ).then_inc(s["bvec_ready"], 1)

        def late_loads(sp):
            sp.dma_start(edge_i[:, 3, :], io["edge_type_8"].rearrange("(p c) -> p c", p=P)).then_inc(s["etype_in"], 16)
            sp.dma_start(weight[:], io["edge_weight"].rearrange("(p c) -> p c", p=P)).then_inc(s["weight_in"], 16)
            for layer in range(2):
                sp.dma_start(comp[:, layer, :], io[f"L3_gnn_comp{layer}"].rearrange("t b -> (t b)").partition_broadcast(P)
                              ).then_inc(s["comp_in"], 16)
            single = ((ROW_BFC, "L2_gnn_bfc"), (ROW_L3B, "L3_gnn_bias0"), (ROW_L3B + 1, "L3_gnn_bias1"))
            double = ((ROW_B1, io["L2_gnn_b1"]), (ROW_B2, io["L2_gnn_b2"]))
            for r, name in single:
                sp.dma_start(rows[r:r + 1, :], row(io[name])).then_inc(s["rows_in"], 16)
            for r, ap in double:
                sp.dma_start(rows[r:r + 2, :], ap.rearrange("(a f) -> a f", a=2)).then_inc(s["rows_in"], 16)
            sp.dma_start(root2, chunked(io["L1_gnn_root2"])).then_inc(s["root2_in"], 16)

        @block.sync
        def _(sp):
            sp.dma_start(x[:], io["x"]).then_inc(s["x_in"], 16)
            for n, w in enumerate((io["L0_gnn_Wq"], io["L0_gnn_Wk"])):
                sp.dma_start(wqk[:, n, :, :], chunked(w)[:, :, D - HD:D]).then_inc(s["wqk_in"], 16)
            for n, name in enumerate(("bq", "bk")):
                sp.dma_start(bqk[:, n, :], row(io[f"L0_gnn_{name}"])[:, D - HD:D]).then_inc(s["bqk_in"], 16)
            sp.dma_start(rows[ROW_BV:ROW_BV + 1, :], row(io["L0_gnn_bv"])).then_inc(s["bias_in"], 16)
            sp.dma_start(wv, chunked(io["L0_gnn_Wv"])).then_inc(s["wv_in"], 16)
            for r in range(2):
                sp.dma_start(rows[ROW_L1B + r:ROW_L1B + r + 1, :], row(io[f"L1_gnn_bias{r + 1}"])).then_inc(s["bias_in"], 16)
            sp.dma_start(root1, chunked(io["L1_gnn_root1"])).then_inc(s["root1_in"], 16)
            for layer, basis in enumerate((io["L1_gnn_basis1"], io["L1_gnn_basis2"])):
                if layer:
                    late_loads(sp)
                view = basis.rearrange("b (t k j h q) o -> t h b k j (q o)", t=TILES, k=BLOCKS, j=GROUPS, h=HALVES)
                with sp.Fori(0, TILES // LOOP_TILES) as it:
                    for slot in range(SLOTS):
                        sp.wait_ge(s["half_free"], it * SLOTS + (layer * TILES * HALVES + slot + 1))
                        tile = view[bass.ds(it * LOOP_TILES + slot // HALVES, 1), slot % HALVES]
                        sp.dma_start(ring[0:BP, slot, :].rearrange("p (j f) -> p j f", j=GROUPS),
                                     tile.rearrange("t b k j f -> (t b) k j f")).then_inc(half_in[slot], 16)

            def slot_free(slot):
                sp.wait_ge(s["half_free"], 2 * TILES * HALVES + slot + 1)

            w1, w2 = chunked(io["L2_gnn_W1"]), chunked(io["L2_gnn_W2"])
            slot_free(0)
            sp.dma_start(W1[:, :, 0:D], w1[:, :, 0:D]).then_inc(s["w1_in"], 16)
            sp.dma_start(W1[:, :, D:GD], w1[:, :, D:GD]).then_inc(s["w1b_in"], 16)
            slot_free(1)
            sp.dma_start(W2[:, 0:4, :], w2[:, 0:4, :]).then_inc(s["w2_in"], 16)
            slot_free(2)
            sp.dma_start(W2[:, 4:8, :], w2[:, 4:8, :]).then_inc(s["w2b_in"], 16)
            slot_free(3)
            sp.dma_start(Wfc, chunked(io["L2_gnn_Wfc"])).then_inc(s["wfc_in"], 16)

            def bases(to, basis, b):
                return sp.dma_start(to, basis[b:b + 2].rearrange("b (k p) f -> p (b k) f", p=P))

            slot_free(4)
            bases(ring[:, 4, :].rearrange("p (c f) -> p c f", c=8), io["L3_gnn_basis0"], 0).then_inc(s["b0a_in"], 16)
            slot_free(5)
            bases(ring[:, 5, :].rearrange("p (c f) -> p c f", c=8), io["L3_gnn_basis0"], 2).then_inc(s["b0b_in"], 16)
            slot_free(6)
            sp.dma_start(conv_w[0][4], chunked(io["L3_gnn_loop0"])).then_inc(s["loops_in"], 16)
            sp.dma_start(conv_w[1][4], chunked(io["L3_gnn_loop1"])).then_inc(s["loops_in"], 16)
            slot_free(7)
            bases(ring[:, 7, :].rearrange("p (c f) -> p c f", c=8), io["L3_gnn_basis1"], 0).then_inc(s["b1a_in"], 16)
            sp.wait_ge(s["proj_done"], 2)
            bases(ring[:, 0, :].rearrange("p (c f) -> p c f", c=8), io["L3_gnn_basis1"], 2).then_inc(s["b1b_in"], 16)

            sp.wait_ge(s["result_ready"], 1)
            sp.dma_start(out, x[:]).then_inc(s["out_done"], 16)
            sp.wait_ge(s["out_done"], 16)

        @block.gpsimd
        def _(pool):
            nc.gpsimd.memset(stat[0:1, 13:14], 0.0).then_inc(s["half_free"], SLOTS)
            nc.gpsimd.memset(stat[0:1, 14:15], 0.0).then_inc(s["contracted"], LOOP_TILES)
            nc.gpsimd.memset(stat[0:1, 15:16], 0.0).then_inc(s["hot_w_used"], 2)
            nc.gpsimd.iota(iota[:], [[1, N]], base=0, channel_multiplier=0,
                           allow_small_or_imprecise_dtypes=True).then_inc(s["iota_ready"], 1)
            nc.gpsimd.memset(ident[:], 0.0).then_inc(s["ident_ready"], 1)
            pool.wait_ge(s["ident_ready"], 1)
            nc.gpsimd.affine_select(out=ident[:], in_=ident[:], compare_op=ALU.not_equal, fill=1.0, base=0,
                                    pattern=[[-1, P]], channel_multiplier=1).then_inc(s["ident_ready"], 1)
            nc.gpsimd.memset(stat[:, NEG_HALF:NEG_HALF + 1], -0.5).then_inc(s["consts_ready"], 1)
            nc.gpsimd.memset(ones[:], 1.0).then_inc(s["consts_ready"], 1)
            nc.gpsimd.memset(uniform[:], 1.0 / N).then_inc(s["consts_ready"], 1)

            rstd_pow(pool, 1)

            nc.gpsimd.memset(mixed[:], 0.0).then_inc(s["mixed_zero"], 1)
            rstd_pow(pool, 2)

            pool.wait_ge(s["coef_ready"], 1)
            pool.wait_ge(s["avec_done"], 8)
            with pool.Fori(0, EC // 2) as it:
                for b in range(2):
                    pool.wait_ge(s["hot_w_used"], it * 2 + (b + 1))
                    nc.gpsimd.tensor_copy(src_c[:, b:b + 1, :], src_hot[:, bass.ds(it * 2 + b, 1), :]
                                          ).then_inc(s["hot_c_ready"], 1)
                    nc.gpsimd.tensor_tensor(
                        work[:, b, :].rearrange("p (c n) -> p c n", n=N),
                        dst_hot[:, bass.ds(it * 2 + b, 1), :].broadcast_to([P, 2 * EB, N]),
                        coef[:, bass.ds(it * 2 + b, 1), :, :].rearrange("p e l b -> p (e l b)").unsqueeze(2)
                        .broadcast_to([P, 2 * EB, N]),
                        ALU.mult).then_inc(s["hot_w_ready"], 1)
            rstd_pow(pool, 3)
            rstd_pow(pool, 4)

        @block.scalar
        def _(act):
            for n, name in enumerate(("src", "dst")):
                act.dma_start(edge_i[:, n, :], io[name].rearrange("(p c) -> p c", p=P)).then_inc(s["edges_in"], 16)
            act.dma_start(edge_i[:, 2, :], io["edge_type_2"].rearrange("(p c) -> p c", p=P)).then_inc(s["rel_in"], 16)

            for layer in range(2):
                act.dma_start(att_rows[layer * NR:(layer + 1) * NR, :], io[f"L1_gnn_att{layer + 1}"]
                              ).then_inc(s["att_in"], 16)
                act.dma_start(gate_rows[layer * NR:(layer + 1) * NR, :],
                              io[f"L1_gnn_gate_w{layer + 1}"].rearrange("r f a -> r (f a)")).then_inc(s["gate_in"], 16)
            for n, name in enumerate(("a_src1", "a_dst1", "a_src2", "a_dst2")):
                act.dma_start(avec_rows[n % 2 * 2:n % 2 * 2 + 2, n // 2, :],
                              io[f"L2_gnn_{name}"].rearrange("g c -> (g c)").rearrange("(a f) -> a f", a=2)
                              ).then_inc(s["avec_in"], 16)
            act.wait_ge(s["qk_done"], 1)
            nc.scalar.copy(qk, bank[5][0:HD, 0:2 * N].rearrange("p (a n) -> p a n", a=2)).then_inc(s["qk_ready"], 1)
            act.wait_ge(s["v_done"], 1)
            nc.scalar.copy(v, bank[6][0:N, :]).then_inc(s["v_ready"], 1)
            act.wait_ge(s["max_ready"], 1)
            nc.scalar.activation(score[:, 1, :], score[:, 0, :], ACT.Exp, bias=stat[:, NEG_MAX:NEG_MAX + 1],
                                 accum_out=stat[:, EXP_SUM:EXP_SUM + 1]).then_inc(s["exp_ready"], 1)

            for layer in range(2):
                act.wait_ge(s["gates_done"], layer + 1)
                nc.scalar.activation(z_exp[:], bank[4][0:N, 0:NR], ACT.Exp, scale=-1.0).then_inc(s["z_ready"], 1)
                act.wait_ge(s["yT_done"], 2 * layer + 1)
                if layer:
                    act.wait_ge(s["y_ready"], TILES)
                nc.scalar.copy(yT[:, 0:4, :], bank[5][:, 0:4 * N].rearrange("p (t n) -> p t n", t=4)
                               ).then_inc(s["yT_a"], 1)
                if layer:
                    biases_out(act, range(0, 2))
                with act.Fori(0, TILES // LOOP_TILES) as it:
                    for u in range(LOOP_TILES):
                        act.wait_ge(s["half_free"], it * SLOTS + (SLOTS + HALVES * (layer * TILES + u + 1)))
                        nc.scalar.copy(w_sb[:, u % 2, :], bank[u % 2][:]).then_inc(s["w_copied"], 1)
                        if layer == 0:
                            act.wait_ge(s["avec_done"], it * LOOP_TILES + (u + 1))
                            nc.scalar.copy(early[0:N, :].rearrange("p (g f) -> p g f", g=8)
                                           [:, bass.ds(it * LOOP_TILES + u, 1), :],
                                           bank[3 + u % 2][0:N, :].unsqueeze(1)).then_inc(s["avec_ready"], 1)

            biases_out(act, range(2, 4))
            for g in range(2):
                for half in range(2):
                    n = 2 * g + half + 1
                    heads = slice(2 * half, 2 * half + 2)
                    act.wait_ge(s["s_masked"], n)
                    nc.scalar.activation(score2[:, heads, :], score[:, heads, :], ACT.Exp).then_inc(s["s_exp"], 1)
                    if half:
                        copy_low(act, g)
                    act.wait_ge(s["alpha_turned"], n)
                    nc.scalar.copy(alphaT[:, heads, :],
                                   bank[6][0:N, 2 * half * N:(2 * half + 2) * N].rearrange("p (g n) -> p g n", g=2)
                                   ).then_inc(s["alphaT_ready"], 1)
                    act.wait_ge(s["gat_rcp"], n)
                    if half == 0:
                        act.wait_ge(s["gat_out"], 3 * g + 1)
                        for head in (0, 1):
                            evacuate(nc.scalar, head).then_inc(s["gat_low_ready"], 1)
                    else:
                        act.wait_ge(s["gat_out"], 3 * g + 3)
                        evacuate(nc.scalar, 3).then_inc(s["gat_h3_ready"], 1)
            for layer in range(2):
                for k in (1, 3):
                    act.wait_ge(s["zT_done"], layer * KC + k + 1)
                    nc.scalar.copy(zT[:, k, :], bank[3 + k][:, 0:5 * N]).then_inc(s["zT_act"], 1)

        @block.vector
        def _(dve):
            def layer_norm(n):
                nc.vector.bn_stats(stat[:, BN:BN + 6], x[:]).then_inc(s["ln_stats"], 1)
                dve.wait_ge(s["ln_stats"], 2 * n - 1)
                nc.vector.bn_aggr(stat[:, MEAN:MEAN + 2], stat[:, BN:BN + 6]).then_inc(s["ln_stats"], 1)
                dve.wait_ge(s["ln_stats"], 2 * n)
                nc.vector.tensor_scalar(stat[:, VAR_EPS:VAR_EPS + 1], stat[:, VAR:VAR + 1], EPS, None, ALU.add
                                        ).then_inc(s["ln_var"], 1)
                nc.vector.tensor_scalar(h[:], x[:], stat[:, MEAN:MEAN + 1], 0.0, ALU.subtract, ALU.max
                                        ).then_inc(s["ln_centred"], 1)
                dve.wait_ge(s["ln_centred"], n)
                dve.wait_ge(s["ln_rstd"], n)
                nc.vector.tensor_scalar(h[:], h[:], stat[:, RSTD:RSTD + 1], None, ALU.mult).then_inc(s["h_ready"], 1)

            def copy_hT(n):
                dve.wait_ge(s["hT_done"], n)
                nc.vector.tensor_copy(hT[:, 0:4, :], bank[3][:, 0:4 * N].rearrange("p (k n) -> p k n", k=4)
                                      ).then_inc(s["hT_ready"], 1)

            dve.wait_ge(s["x_in"], 16)
            layer_norm(1)
            dve.wait_ge(s["edges_in"], 32)
            nc.vector.tensor_copy(edge_f[:, 0:2, :], edge_i[:, 0:2, :]).then_inc(s["edges_float"], 1)
            dve.wait_ge(s["rel_in"], 16)
            nc.vector.tensor_copy(edge_f[:, 2, :], edge_i[:, 2, :]).then_inc(s["edges_float"], 1)
            dve.wait_ge(s["edges_float"], 2)
            nc.vector.tensor_scalar(is_rel0[:], edge_f[:, 2, :], 0.0, None, ALU.is_equal).then_inc(s["edges_float"], 1)

            dve.wait_ge(s["iota_ready"], 1)
            every_node = iota[:].unsqueeze(1).broadcast_to([P, EC, N])
            for n, hot in enumerate((src_hot, dst_hot)):
                nc.vector.tensor_tensor(hot, edge_f[:, n, :].unsqueeze(2).broadcast_to([P, EC, N]), every_node,
                                        ALU.is_equal).then_inc(s["hots_ready"], 1)
            dve.wait_ge(s["edges_float"], 3)
            dve.wait_ge(s["hots_ready"], 2)
            nc.vector.tensor_tensor(src_hot0, src_hot, is_rel0[:].unsqueeze(2).broadcast_to([P, EC, N]),
                                    ALU.mult).then_inc(s["hot0_ready"], 1)
            dve.wait_ge(s["ident_ready"], 2)
            nc.vector.tensor_reduce(same_block[:], ident[0:BP, 0:BP].rearrange("p (b k) -> p k b", k=BLOCKS), X, ALU.add
                                    ).then_inc(s["block_ready"], 1)
            nc.vector.memset(att_w[:], 0.0).then_inc(s["attw_zero"], 1)
            copy_hT(1)

            dve.wait_ge(s["counts_done"], 1)
            nc.vector.tensor_scalar(has_edge[:], bank[4][0:N, 0:N], 0.0, None, ALU.is_gt).then_inc(s["edge_mask"], 1)
            nc.vector.tensor_copy(relT[:, 0, :], bank[4][0:N, 2 * N:3 * N]).then_inc(s["rel_ready"], 1)
            nc.vector.tensor_tensor(gat_count[:], bank[4][0:N, N:2 * N], ident[0:N, 0:N], ALU.add
                                    ).then_inc(s["gat_mask"], 1)
            dve.wait_ge(s["rel_ready"], 1)
            nc.vector.tensor_tensor(relT[:, 1, :], bank[4][0:N, N:2 * N], relT[:, 0, :], ALU.subtract
                                    ).then_inc(s["rel_ready"], 1)
            dve.wait_ge(s["gat_mask"], 1)
            nc.vector.tensor_scalar(absent[:], gat_count[:], 0.0, ABSENT, ALU.is_equal, ALU.mult
                                    ).then_inc(s["gat_mask"], 1)

            dve.wait_ge(s["att_in"], 32)
            nc.vector.tensor_copy(expand, att_rows[:].unsqueeze(2).broadcast_to([2 * NR, NB, BLOCKS])
                                  ).then_inc(s["expand_ready"], 1)

            dve.wait_ge(s["scores_done"], 1)
            dve.wait_ge(s["edge_mask"], 1)
            nc.vector.scalar_tensor_tensor(out=score[:, 0, :], in0=bank[7][0:N, 0:N], scalar=float(HD) ** -0.5,
                                           in1=has_edge[:], op0=ALU.mult, op1=ALU.mult).then_inc(s["masked"], 1)
            dve.wait_ge(s["masked"], 1)
            nc.vector.tensor_reduce(stat[:, NEG_MAX:NEG_MAX + 1], score[:, 0, :], X, ALU.max, negate=True
                                    ).then_inc(s["max_ready"], 1)
            dve.wait_ge(s["exp_ready"], 1)
            nc.vector.reciprocal(stat[:, EXP_RCP:EXP_RCP + 1], stat[:, EXP_SUM:EXP_SUM + 1]).then_inc(s["masked"], 1)
            dve.wait_ge(s["masked"], 2)
            nc.vector.tensor_scalar(score[:, 1, :], score[:, 1, :], stat[:, EXP_RCP:EXP_RCP + 1], None, ALU.mult
                                    ).then_inc(s["att_norm"], 1)
            dve.wait_ge(s["att_turned"], 1)
            nc.vector.tensor_copy(alphaT[:, 0, :], bank[3][0:N, 0:N]).then_inc(s["att_turned_ready"], 1)
            dve.wait_ge(s["attn_done"], 1)
            nc.vector.tensor_tensor(x[:], x[:], bank[5][0:N, :], ALU.add).then_inc(s["x_ready"], 1)
            dve.wait_ge(s["x_ready"], 1)
            layer_norm(2)

            dve.wait_ge(s["attp_done"], 1)
            nc.vector.tensor_copy(att_p[:], bank[7][0:BP, 0:2 * NR]).then_inc(s["attp_ready"], 1)
            dve.wait_ge(s["attp_ready"], 1)
            dve.wait_ge(s["block_ready"], 1)
            dve.wait_ge(s["attw_zero"], 1)
            for layer in range(2):
                for r in range(NR):
                    nc.vector.tensor_scalar(
                        att_w[:, layer, :].rearrange("p (q c) -> p q c", q=STEPS)[:, :, 4 * r:4 * r + 4],
                        same_block[:].unsqueeze(1).broadcast_to([BP, STEPS, BLOCKS]),
                        att_p[:, layer * NR + r:layer * NR + r + 1], None, ALU.mult).then_inc(s["attw_ready"], 1)
            dve.wait_ge(s["gateT_done"], 1)
            nc.vector.tensor_copy(gateT[:], bank[6][:, 0:KC * 2 * NR].rearrange("p (k g) -> p k g", k=KC)
                                  ).then_inc(s["gateT_ready"], 1)

            for layer in range(2):
                copy_hT(2 + layer)
                dve.wait_ge(s["z_ready"], layer + 1)
                nc.vector.tensor_scalar(gate[:], z_exp[:], 1.0, None, ALU.add).then_inc(s["gate_p1"], 1)
                dve.wait_ge(s["gate_p1"], layer + 1)
                nc.vector.reciprocal(gate[:], gate[:]).then_inc(s["gate_ready"], 1)
                dve.wait_ge(s["gate_ready"], layer + 1)
                dve.wait_ge(s["mixed_zero"], 1)
                for r in range(NR):
                    nc.vector.tensor_scalar(
                        mixed[:, r, :].rearrange("p (t s r k) -> p t s r k", t=TILES, r=NR, k=BLOCKS)[:, :, :, r, :],
                        h[:].rearrange("p (t k s) -> p t s k", t=TILES, k=BLOCKS),
                        gate[:, r:r + 1], None, ALU.mult).then_inc(s["mixed_ready"], 1)
                dve.wait_ge(s["yT_done"], 2 * layer + 2)
                nc.vector.tensor_copy(yT[:, 4:8, :], bank[6][:, 0:4 * N].rearrange("p (t n) -> p t n", t=4)
                                      ).then_inc(s["yT_ready"], 1)
                if layer:
                    edge_coefficients(dve)
                dve.wait_ge(s["yT_a"], layer + 1)
                dve.wait_ge(s["yT_ready"], layer + 1)
                with dve.Fori(0, TILES // LOOP_TILES) as it:
                    for u in range(LOOP_TILES):
                        dve.wait_ge(s["contracted"], it * LOOP_TILES + (layer * TILES + u + 1))
                        nc.vector.tensor_copy(y_now[:, u:u + 1, :], yT[:, bass.ds(it * LOOP_TILES + u, 1), :]
                                              ).then_inc(s["y_ready"], 1)
                dve.wait_ge(s["contracted"], LOOP_TILES + (layer + 1) * TILES)
                if layer == 0:
                    nc.vector.tensor_scalar(h[:], bank[2][0:N, :], 0.0, None, ALU.max).then_inc(s["h_ready"], 1)
                else:
                    nc.vector.tensor_tensor(x[:], x[:], bank[2][0:N, :], ALU.add).then_inc(s["x_ready"], 1)
                    dve.wait_ge(s["x_ready"], 2)
                    layer_norm(3)

            for g in range(2):
                if g == 0:
                    copy_hT(4)
                    for n in range(2):
                        dve.wait_ge(s["hot_w_used"], 2 + EC)
                        nc.vector.tensor_copy(mix3[:, n, 0:EB * N], bank[6 + n][0:N, 0:EB * N]).then_inc(s["mix_ready"], 1)
                        nc.vector.tensor_copy(mix3[:, n, EB * N:], ident[0:N, 0:N]).then_inc(s["mix_ready"], 1)
                for half in range(2):
                    gat_softmax(dve, g, half)
                dve.wait_ge(s["gat_rcp"], 2 * g + 2)
                dve.wait_ge(s["gat_out"], 3 * g + 2)
                evacuate(nc.vector, 2).then_inc(s["gat_h2_ready"], 1)
                dve.wait_ge(s["high_done"], g + 1)
                nc.vector.tensor_copy(hT[:, 4:8, :], bank[3][:, 0:4 * N].rearrange("p (k n) -> p k n", k=4)
                                      ).then_inc(s["high_ready"], 1)

            dve.wait_ge(s["fc_done"], 1)
            nc.vector.tensor_tensor(x[:], x[:], bank[0][0:N, :], ALU.add).then_inc(s["x_ready"], 1)
            dve.wait_ge(s["x_ready"], 3)
            layer_norm(4)
            for layer in range(2):
                for k in (0, 2):
                    dve.wait_ge(s["zT_done"], layer * KC + k + 1)
                    nc.vector.tensor_copy(zT[:, k, :], bank[3 + k][:, 0:5 * N]).then_inc(s["zT_dve"], 1)
                dve.wait_ge(s["conv_done"], layer + 1)
                if layer == 0:
                    nc.vector.tensor_scalar(h[:], bank[7][0:N, :], 0.0, None, ALU.max).then_inc(s["h_ready"], 1)
                else:
                    nc.vector.tensor_tensor(x[:], x[:], bank[2][0:N, :], ALU.add).then_inc(s["result_ready"], 1)

        @block.tensor
        def _(pe):
            def transposes(source, n, to, done):
                for k in range(4):
                    c = (n + k) * P
                    mm = nc.tensor.transpose(to[:, k * N:(k + 1) * N], source[:, c:c + P], ident[0:N, 0:N])
                mm.then_inc(s[done], 1)

            pe.wait_ge(s["ident_ready"], 2)
            pe.wait_ge(s["h_ready"], 1)
            transposes(h, 0, bank[3], "hT_done")
            pe.wait_ge(s["hT_ready"], 1)
            pe.wait_ge(s["wqk_in"], 32)
            pe.wait_ge(s["bqk_in"], 32)
            pe.wait_ge(s["consts_ready"], 3)
            for n in range(2):
                q_ps = bank[5][0:HD, n * N:(n + 1) * N]
                nc.tensor.matmul(q_ps, bqk[:, n, :], ones[0:1, :], start=True, stop=False)
                for k in range(KC):
                    mm = nc.tensor.matmul(q_ps, wqk[:, n, k, :], hT[:, k, :], start=False, stop=(k == KC - 1))
            mm.then_inc(s["qk_done"], 1)
            pe.wait_ge(s["hots_ready"], 2)
            pe.wait_ge(s["hot0_ready"], 1)
            for n, (left, right) in enumerate(((src_hot, dst_hot), (dst_hot, src_hot), (dst_hot, src_hot0))):
                for c in range(EC):
                    mm = nc.tensor.matmul(bank[4][0:N, n * N:(n + 1) * N], left[:, c, :], right[:, c, :],
                                          start=(c == 0), stop=(c == EC - 1))
            mm.then_inc(s["counts_done"], 1)
            pe.wait_ge(s["qk_ready"], 1)
            nc.tensor.matmul(bank[7][0:N, 0:N], qk[:, 0, :], qk[:, 1, :], start=True, stop=True).then_inc(s["scores_done"], 1)
            pe.wait_ge(s["bias_in"], 48)
            nc.tensor.matmul(bank[6][0:N, :], ones[0:1, :], rows[0:1, :], start=True, stop=False)
            pe.wait_ge(s["wv_in"], 16)
            for k in range(KC):
                mm = nc.tensor.matmul(bank[6][0:N, :], hT[:, k, :], wv[:, k, :], start=False, stop=(k == KC - 1))
            mm.then_inc(s["v_done"], 1)
            pe.wait_ge(s["v_ready"], 1)
            pe.wait_ge(s["gate_in"], 32)
            for k in range(KC):
                mm = nc.tensor.transpose(bank[6][:, k * 2 * NR:(k + 1) * 2 * NR], gate_rows[:, k * P:(k + 1) * P],
                                         ident[0:2 * NR, 0:2 * NR])
            mm.then_inc(s["gateT_done"], 1)
            pe.wait_ge(s["att_norm"], 1)
            nc.tensor.transpose(bank[3][0:N, 0:N], score[:, 1, :], ident[0:N, 0:N]).then_inc(s["att_turned"], 1)
            pe.wait_ge(s["expand_ready"], 1)
            nc.tensor.transpose(bank[7][0:BP, 0:2 * NR], expand.rearrange("p b k -> p (b k)"),
                                ident[0:2 * NR, 0:2 * NR]).then_inc(s["attp_done"], 1)
            pe.wait_ge(s["att_turned_ready"], 1)
            nc.tensor.matmul(bank[5][0:N, 0:D - HD], uniform[:], v[:, 0:D - HD], start=True, stop=True)
            nc.tensor.matmul(bank[5][0:N, D - HD:D], alphaT[:, 0, :], v[:, D - HD:D], start=True, stop=True
                             ).then_inc(s["attn_done"], 1)

            for layer in range(2):
                pe.wait_ge(s["h_ready"], 2 + layer)
                transposes(h, 0, bank[3], "hT_done")
                pe.wait_ge(s["hT_ready"], 2 + layer)
                pe.wait_ge(s["gateT_ready"], 1)
                pe.wait_ge(s["gat_mask"], 2)
                for k in range(KC):
                    mm = nc.tensor.matmul(bank[4][0:N, 0:NR], hT[:, k, :], gateT[:, k, layer * NR:(layer + 1) * NR],
                                          start=(k == 0), stop=(k == KC - 1))
                mm.then_inc(s["gates_done"], 1)
                pe.wait_ge(s["bias_in"], 48)
                nc.tensor.matmul(bank[2][0:N, :], pick(ROW_L1B + layer, ROW_B1), rows[0:ROW_B1, :], start=True, stop=True,
                                 skip_group_check=True)
                pe.wait_ge(s[f"root{layer + 1}_in"], 16)
                root = (root1, root2)[layer]
                for k in range(KC):
                    nc.tensor.matmul(bank[2][0:N, :], hT[:, k, :], root[:, k, :], start=False, stop=True,
                                     skip_group_check=True)
                pe.wait_ge(s["mixed_ready"], 2 * (layer + 1))
                pe.wait_ge(s["rel_ready"], 2)
                for t in range(TILES):
                    y_ps = bank[5 + t // 4][:, (t % 4) * N:(t % 4 + 1) * N]
                    for r in range(NR):
                        mm = nc.tensor.matmul(y_ps, mixed[:, r, t * P:(t + 1) * P], relT[:, r, :],
                                              start=(r == 0), stop=(r == NR - 1))
                    if t % 4 == 3:
                        mm.then_inc(s["yT_done"], 1)
                pe.wait_ge(s["attw_ready"], 4)
                if layer == 0:
                    pe.wait_ge(s["avec_in"], 64)
                else:
                    pe.wait_ge(s["rows_in"], 16 * 5)
                    gat_biases(pe, range(0, 2))
                    open_edge_mixes(pe)
                rounds = TILES // LOOP_TILES
                mixes = ((0,), (1, 2), (3,), (4,))
                with pe.Fori(0, rounds) as it:
                    for u in range(LOOP_TILES):
                        basis_product(pe, layer, it, u, 0)
                        if u:
                            contract(pe, layer, it, u - 1)
                        if layer == 0:
                            gat_vector(pe, it, u)
                        else:
                            for n in mixes[u]:
                                edge_mix(pe, it * (EC // rounds) + n, n % 2)
                        basis_product(pe, layer, it, u, 1)
                    contract(pe, layer, it, LOOP_TILES - 1)
                    if layer:
                        edge_mix(pe, it * (EC // rounds) + EC // rounds - 1, 1)
                if layer == 0:
                    pe.wait_ge(s["avec_ready"], 8)

            def keep_clock(n, b):
                for _ in range(n):
                    nc.tensor.matmul(bank[b][0:N, :], src_hot[:, 0, :], hots[:, 1].rearrange("p e n -> p (e n)")[:, 0:D],
                                     start=True, stop=True)

            def proj(g, half, ks, first, last):
                W = (W1, W2)[g]
                for k in ks:
                    mm = nc.tensor.matmul(gat_bank(g, half)[0:N, :], hT[:, k, :], W[:, k, half * D:(half + 1) * D],
                                          start=(k == first), stop=(k == last))
                if ks[-1] == last:
                    mm.then_inc(s["proj_done"], 1)

            def fc(ks):
                for k in ks:
                    mm = nc.tensor.matmul(bank[0][0:N, :], hT[:, k, :], Wfc[:, k, :], start=False, stop=(k == 7))
                if ks[-1] == 7:
                    mm.then_inc(s["fc_done"], 1)

            def source_scores(g, half):
                n = 2 * g + half + 1
                pe.wait_ge(s["diag_ready"], n)
                nc.tensor.matmul(bank[5][0:N, 2 * half * N:(2 * half + 2) * N], ones[:],
                                 score[:, 2 * half:2 * half + 2, :].rearrange("p g n -> p (g n)"),
                                 start=True, stop=True).then_inc(s["e_done"], 1)

            def turn_weights(g, half):
                pe.wait_ge(s["alpha_ready"], 2 * g + half + 1)
                for head in (2 * half, 2 * half + 1):
                    mm = nc.tensor.transpose(bank[6][0:N, head * N:(head + 1) * N], score2[:, head, :], ident[0:N, 0:N])
                mm.then_inc(s["alpha_turned"], 1)

            def weigh(g, half):
                pe.wait_ge(s["alphaT_ready"], 2 * g + half + 1)
                pe.wait_ge(s["gat_h_ready"], 2 * g + half + 1)
                if half:
                    pe.wait_ge(s["gat_low_ready"], 2 * (g + 1))
                for head in (2 * half, 2 * half + 1):
                    ps = (bank[4], bank[4], bank[4], bank[5])[head]
                    mm = nc.tensor.matmul(ps[0:N, head % 2 * GC:(head % 2 + 1) * GC], alphaT[:, head, :],
                                          gat_h[:, head * GC:(head + 1) * GC], start=True, stop=True)
                    if head:
                        mm.then_inc(s["gat_out"], 1)

            gat_biases(pe, range(2, 4))
            pe.wait_ge(s["h_ready"], 4)
            transposes(h, 0, bank[3], "hT_done")
            keep_clock(3, 2)
            pe.wait_ge(s["hT_ready"], 4)
            pe.wait_ge(s["w1_in"], 16)
            proj(0, 0, range(0, 4), 0, 3)
            pe.wait_ge(s["w1b_in"], 16)
            proj(0, 1, range(0, 2), 0, 3)
            pe.wait_ge(s["bvec_ready"], 4)
            source_scores(0, 0)
            proj(0, 1, range(2, 4), 0, 3)
            for g in range(2):
                spare = 2 - g
                keep_clock(5, spare)
                turn_weights(g, 0)
                keep_clock(3, spare)
                source_scores(g, 1)
                weigh(g, 0)
                keep_clock(4, spare)
                pe.wait_ge(s["gat_low_ready"], 2 * (g + 1))
                transposes(gat_o, 0, bank[3], "low_done")
                if g == 0:
                    keep_clock(4, spare)
                if g:
                    nc.tensor.matmul(bank[0][0:N, :], pick(ROW_BFC), rows[:], start=True, stop=False)
                turn_weights(g, 1)
                pe.wait_ge(s["low_ready"], g + 1)
                if g == 0:
                    pe.wait_ge(s["w2_in"], 16)
                    pe.wait_ge(s["mix_ready"], 4)
                    proj(1, 0, range(0, 1), 0, 7)
                else:
                    pe.wait_ge(s["wfc_in"], 16)
                    fc(range(0, 1))
                weigh(g, 1)
                if g == 0:
                    proj(1, 0, range(1, 4), 0, 7)
                else:
                    fc(range(1, 4))
                pe.wait_ge(s["gat_h2_ready"], g + 1)
                pe.wait_ge(s["gat_h3_ready"], g + 1)
                transposes(gat_o, 4, bank[3], "high_done")
                keep_clock(3, spare)
                pe.wait_ge(s["high_ready"], g + 1)
                if g == 0:
                    pe.wait_ge(s["w2b_in"], 16)
                    proj(1, 0, range(4, 8), 0, 7)
                    proj(1, 1, range(0, 4), 0, 7)
                    source_scores(1, 0)
                    proj(1, 1, range(4, 8), 0, 7)
                else:
                    fc(range(4, 8))

            for layer in range(2):
                ps = (bank[7], bank[2])[layer]
                nc.tensor.matmul(ps[0:N, :], pick(ROW_L3B + layer), rows[:], start=True, stop=False)
                if layer == 0:
                    keep_clock(10, 1)
                pe.wait_ge(s["h_ready"], 5 + layer)
                pe.wait_ge(s["mix_ready"], 4)
                for k in range(KC):
                    nc.tensor.matmul(bank[3 + k][:, 0:5 * N], h[:, k * P:(k + 1) * P], mix3[:, layer, :],
                                     start=True, stop=True).then_inc(s["zT_done"], 1)
                for name in (("b0a_in", "b0b_in"), ("b1a_in", "b1b_in"))[layer]:
                    pe.wait_ge(s[name], 16)
                pe.wait_ge(s["loops_in"], 32)
                for k in range(KC):
                    pe.wait_ge(s[("zT_dve", "zT_act")[k % 2]], 2 * layer + k // 2 + 1)
                    for b in range(EB + 1):
                        mm = nc.tensor.matmul(ps[0:N, :], zT[:, k, b * N:(b + 1) * N], conv_w[layer][b][:, k, :],
                                              start=False, stop=(k == KC - 1 and b == EB))
                mm.then_inc(s["conv_done"], 1)


_OUTS = [((N, D), "float32")]


def kernel(**inputs):
    import numpy as _np
    import concourse.bacc as _bacc
    from concourse import mybir as _mybir
    from concourse.bass_utils import run_bass_kernel_spmd as _run

    nc = _bacc.Bacc("TRN2", target_bir_lowering=False, num_devices=1)
    arrays, io = {}, {}
    for name in inputs:
        a = _np.ascontiguousarray(inputs[name])
        arrays[f"in_{name}_dram"] = a
        io[name] = nc.dram_tensor(f"in_{name}_dram", a.shape, _mybir.dt.from_np(a.dtype), kind="ExternalInput").ap()
    shape, dtype = _OUTS[0]
    result = nc.dram_tensor("out_0_dram", shape, _mybir.dt.from_np(_np.dtype(dtype)), kind="ExternalOutput").ap()
    gnn_blocks(nc, io, result)
    r = _run(nc, [arrays], core_ids=[0])
    return r.results[0]["out_0_dram"]
```

```python
from contextlib import ExitStack

import concourse.bass as bass
from concourse import mybir

F32 = mybir.dt.float32
BF16 = mybir.dt.bfloat16
I32 = mybir.dt.int32
ALU = mybir.AluOpType
ACT = mybir.ActivationFunctionType
X = mybir.AxisListType.X

N = 96
D = 512
E = 1536
P = 128
EC = E // P
KC = D // P
HEADS, HD = 8, 64
NB, NR = 30, 2
BLOCKS = 4
BP = NB * BLOCKS
GROUPS, STEPS = 4, 4
TILE = BLOCKS * GROUPS * STEPS
TILES = D // TILE
HALVES = 2
SLOTS = 8
LOOP_TILES = SLOTS // HALVES
GH, GC = 4, 256
GD = GH * GC
ET, EB = 8, 4
EPS = 1e-5
ABSENT = -1e30

ROW_BV, ROW_L1B, ROW_B1, ROW_B2, ROW_BFC, ROW_L3B = 0, 1, 3, 5, 7, 8
ROWS = 10


def gnn_blocks(nc, io, out):
    with ExitStack() as ctx:
        def sb(name, shape, dt=F32):
            return ctx.enter_context(nc.sbuf_tensor(name, shape, dt))

        def sem(name):
            return ctx.enter_context(nc.semaphore(name))

        ring = sb("ring", [P, SLOTS, 8 * D])
        early = sb("early", [P, 8 * D])
        wv = early[:, 0:4 * D].rearrange("p (k f) -> p k f", k=KC)
        root1 = early[:, 4 * D:8 * D].rearrange("p (k f) -> p k f", k=KC)
        avec = early[0:N, :].rearrange("p (g f) -> p g f", g=4)
        late = sb("late", [P, KC * 5 * N + 128])
        root2 = late[:, 0:4 * D].rearrange("p (k f) -> p k f", k=KC)
        bvec = late[0:N, :].rearrange("p (g f) -> p g f", g=2)
        zT = late[:, 0:KC * 5 * N].rearrange("p (k f) -> p k f", k=KC)
        wqk = sb("wqk", [P, 2, KC, HD])
        mixed = sb("mixed", [N, NR, TILES * P])
        gat_h = mixed[:, 0, :]
        gat_o = mixed[:, 1, :]
        yT = sb("yT", [P, TILES, N])
        y_now = sb("y_now", [P, LOOP_TILES, N])
        w_sb = sb("w_sb", [P, 2, D])
        x = sb("x", [N, D])
        h = sb("h", [N, D])
        hT = sb("hT", [P, 8, N])
        v = yT[0:N].rearrange("p t n -> p (t n)")[:, 0:D]
        qk = y_now[0:HD, 0:2, :]
        ident = sb("ident", [P, P])
        iota = sb("iota", [P, N])
        ones = sb("ones", [N, N])
        uniform = sb("uniform", [N, N])
        rows = sb("rows", [ROWS, D])
        bqk = sb("bqk", [1, 2, HD])
        gate_rows = sb("gate_rows", [2 * NR, D])
        gateT = sb("gateT", [P, KC, 2 * NR])
        edge_i = sb("edge_i", [P, 4, EC], I32)
        edge_f = sb("edge_f", [P, 4, EC])
        weight = sb("weight", [P, EC])
        comp = sb("comp", [P, 2, ET * EB])
        att_rows = sb("att_rows", [2 * NR, NB])
        att_p = sb("att_p", [BP, 2 * NR])
        same_block = sb("same_block", [BP, BLOCKS])
        att_w = sb("att_w", [BP, 2, 160])
        edge_area = sb("edge_area", [P, 3 * EC * N // 2])
        hots = edge_area[:].bitcast(BF16).rearrange("p (a e n) -> p a e n", a=3, e=EC)
        src_hot, dst_hot, src_hot0 = hots[:, 0], hots[:, 1], hots[:, 2]
        src_c = sb("src_c", [P, 2, N])
        mix3 = sb("mix3", [N, 2, 5 * N])
        is_rel0 = sb("is_rel0", [P, EC])
        has_edge = sb("has_edge", [N, N])
        relT = sb("relT", [N, NR, N])
        gat_count = sb("gat_count", [N, N])
        absent = sb("absent", [N, N])
        is_type = sb("is_type", [P, EC, ET])
        typed = sb("typed", [P, EC, EB, ET])
        coef = sb("coef", [P, EC, 2, EB])
        work = sb("work", [P, 2, 2 * EB * N])
        score = work[0:N, 0, 0:GH * N].rearrange("p (g s) -> p g s", g=GH)
        score2 = work[0:N, 0, GH * N:2 * GH * N].rearrange("p (g s) -> p g s", g=GH)
        alphaT = work[0:N, 1, 0:GH * N].rearrange("p (g s) -> p g s", g=GH)
        dot_out = [work[0:N, 1, GH * N:GH * N + GC], typed[0:N].rearrange("p e b t -> p (e b t)")[:, 0:GC]]
        expand = work[0:2 * NR, 1, GH * N + GC:GH * N + GC + BP].rearrange("p (b k) -> p b k", b=NB)
        avec_rows = work[0:LOOP_TILES].rearrange("p a f -> p (a f)")[:, 2 * N:16 * N].rearrange(
            "p (i f) -> p i f", i=2)[:, :, 0:D]
        al = sb("al", [N, 2, GH])
        stat = sb("stat", [N, 44])
        z_exp = sb("z_exp", [N, NR])
        gate = sb("gate", [N, NR])
        bank = [ctx.enter_context(nc.psum_tensor(f"bank{i}", [P, D], F32)) for i in range(8)]

        W1 = ring[:, 0, :].rearrange("p (k f) -> p k f", k=4)
        W2 = ring[:, 1:3, :].rearrange("p s (k f) -> p (s k) f", k=4)
        Wfc = ring[:, 3, :].rearrange("p (k f) -> p k f", k=8)
        conv_w = [[ring[:, slot, c * 4 * D:(c + 1) * 4 * D].rearrange("p (k f) -> p k f", k=KC) for slot, c in at]
                  for at in (((4, 0), (4, 1), (5, 0), (5, 1), (6, 0)), ((7, 0), (7, 1), (0, 0), (0, 1), (6, 1)))]

        names = """x_in edges_in rel_in wqk_in wv_in bias_in bqk_in rows_in avec_in gate_in att_in etype_in weight_in comp_in
            root1_in root2_in w1_in w1b_in w2_in w2b_in wfc_in b0a_in b0b_in loops_in b1a_in b1b_in out_done
            ident_ready iota_ready consts_ready edges_float hots_ready hot0_ready
            half_free w_copied y_ready contracted
            counts_done rel_ready edge_mask gat_mask
            ln_stats ln_var ln_rstd ln_centred h_ready hT_done hT_ready low_done low_ready high_done high_ready
            qk_done qk_ready v_done v_ready scores_done masked max_ready exp_ready att_norm att_turned att_turned_ready
            attn_done x_ready
            expand_ready attp_done attp_ready block_ready attw_zero attw_ready gateT_done gateT_ready
            gates_done z_ready gate_p1 gate_ready mixed_zero mixed_ready yT_done yT_a yT_ready
            coef_steps coef_ready hot_c_ready hot_w_ready hot_w_used mix_ready
            avec_done avec_ready
            bvec_done bvec_ready proj_done src_dots dst_dots diag_ready e_done softmax_step s_masked s_exp
            gat_h_ready alpha_ready gat_rcp alpha_turned alphaT_ready
            gat_out gat_low_ready gat_h2_ready gat_h3_ready
            fc_done zT_done zT_dve zT_act conv_done result_ready""".split()
        s = {n: sem(n) for n in names}
        half_in = [sem(f"half_in{i}") for i in range(SLOTS)]

        block = ctx.enter_context(nc.Block())

        def row(ap):
            return ap.rearrange("(a f) -> a f", a=1)

        def chunked(w):
            return w.rearrange("(k p) f -> p k f", p=P)

        BN, MEAN, VAR, VAR_EPS, RSTD, NEG_MAX, EXP_SUM, EXP_RCP, NEG_HALF = 32, 6, 7, 10, 11, 8, 9, 12, 16
        GAT_MAX, GAT_SUM, GAT_RCP = 20, 24, 28

        def pick(r, of=ROWS):
            return ident[0:of, r:r + 1].broadcast_to([of, N])

        def rstd_pow(pool, n):
            pool.wait_ge(s["consts_ready"], 1)
            pool.wait_ge(s["ln_var"], n)
            nc.gpsimd.tensor_tensor(stat[:, RSTD:RSTD + 1], stat[:, VAR_EPS:VAR_EPS + 1],
                                    stat[:, NEG_HALF:NEG_HALF + 1], ALU.pow).then_inc(s["ln_rstd"], 1)

        def copy_low(act, g):
            act.wait_ge(s["low_done"], g + 1)
            nc.scalar.copy(hT[:, 0:4, :], bank[3][:, 0:4 * N].rearrange("p (k n) -> p k n", k=4)
                           ).then_inc(s["low_ready"], 1)

        def evacuate(engine, head):
            to = gat_o[:, head * GC:(head + 1) * GC]
            ps = (bank[4], bank[4], bank[4], bank[5])[head][0:N, head % 2 * GC:(head % 2 + 1) * GC]
            scale = stat[:, GAT_RCP + head:GAT_RCP + head + 1]
            if engine is nc.scalar:
                return engine.activation(to, ps, ACT.Relu, scale=scale)
            return engine.tensor_scalar(to, ps, scale, 0.0, ALU.mult, ALU.max)

        def edge_coefficients(dve):
            dve.wait_ge(s["etype_in"], 16)
            dve.wait_ge(s["comp_in"], 32)
            dve.wait_ge(s["weight_in"], 16)
            nc.vector.tensor_copy(edge_f[:, 3, :], edge_i[:, 3, :]).then_inc(s["coef_steps"], 1)
            dve.wait_ge(s["coef_steps"], 1)
            nc.vector.tensor_tensor(is_type[:], edge_f[:, 3, :].unsqueeze(2).broadcast_to([P, EC, ET]),
                                    iota[:, 0:ET].unsqueeze(1).broadcast_to([P, EC, ET]), ALU.is_equal
                                    ).then_inc(s["coef_steps"], 1)
            dve.wait_ge(s["coef_steps"], 2)
            for layer in range(2):
                nc.vector.tensor_tensor(
                    typed[:], is_type[:].unsqueeze(2).broadcast_to([P, EC, EB, ET]),
                    comp[:, layer, :].rearrange("p (t b) -> p b t", t=ET).unsqueeze(1).broadcast_to([P, EC, EB, ET]),
                    ALU.mult).then_inc(s["coef_steps"], 1)
                dve.wait_ge(s["coef_steps"], 3 + 2 * layer)
                nc.vector.tensor_reduce(coef[:, :, layer, :], typed[:], X, ALU.add).then_inc(s["coef_steps"], 1)
                dve.wait_ge(s["coef_steps"], 4 + 2 * layer)
            both = coef[:].rearrange("p e l b -> p e (l b)")
            nc.vector.tensor_tensor(both, both, weight[:].unsqueeze(2).broadcast_to([P, EC, 2 * EB]), ALU.mult
                                    ).then_inc(s["coef_ready"], 1)

        def gat_softmax(dve, g, half):
            n = 2 * g + half + 1
            heads = slice(2 * half, 2 * half + 2)
            both = (2 * half, 2 * half + 1)
            sc, sc2 = score[:, heads, :], score2[:, heads, :]

            def step(ins, k):
                ins.then_inc(s["softmax_step"], 1)
                dve.wait_ge(s["softmax_step"], 2 * (n - 1) + k)

            def per_head(ap):
                return ap.unsqueeze(2).broadcast_to([N, 2, N])

            def every_head(ap):
                return ap.unsqueeze(1).broadcast_to([N, 2, N])

            def dots(side, done):
                for head in both:
                    nc.vector.tensor_tensor_reduce(
                        out=dot_out[head % 2], in0=gat_bank(g, half)[0:N, head % 2 * GC:(head % 2 + 1) * GC],
                        in1=avec[:, 2 * g + side, head * GC:(head + 1) * GC], scale=1.0, scalar=0.0,
                        op0=ALU.mult, op1=ALU.add, accum_out=al[:, side, head:head + 1]).then_inc(s[done], 1)

            dve.wait_ge(s["avec_ready"], 8)
            dve.wait_ge(s["bvec_ready"], 4)
            dve.wait_ge(s["proj_done"], n)
            if n > 1:
                dve.wait_ge(s["dst_dots"], 2 * (n - 1))
            dots(0, "src_dots")
            dve.wait_ge(s["src_dots"], 2 * n)
            nc.vector.tensor_tensor(sc, every_head(ident[0:N, 0:N]), per_head(al[:, 0, heads]), ALU.mult
                                    ).then_inc(s["diag_ready"], 1)
            dots(1, "dst_dots")
            dve.wait_ge(s["dst_dots"], 2 * n)
            dve.wait_ge(s["e_done"], n)
            from_src = bank[5][0:N, 2 * half * N:(2 * half + 2) * N].rearrange("p (g n) -> p g n", g=2)
            step(nc.vector.tensor_tensor(sc, from_src,
                                         per_head(al[:, 1, heads]), ALU.add), 1)
            step(nc.vector.scalar_tensor_tensor(out=sc2, in0=sc, scalar=0.2, in1=sc, op0=ALU.mult, op1=ALU.max), 2)
            for head in both:
                nc.vector.tensor_tensor_reduce(
                    out=score[:, head, :], in0=score2[:, head, :], in1=absent[:], scale=-1.0, scalar=-2 * ABSENT,
                    op0=ALU.add, op1=ALU.min, accum_out=stat[:, GAT_MAX + head:GAT_MAX + head + 1]
                    ).then_inc(s["s_masked"], 1)
            cols = slice(half * D, (half + 1) * D)
            nc.vector.tensor_tensor(gat_h[:, cols], gat_bank(g, half)[0:N, :], bvec[:, g, cols], ALU.add
                                    ).then_inc(s["gat_h_ready"], 1)
            for m, head in enumerate(both):
                dve.wait_ge(s["s_exp"], 2 * (n - 1) + m + 1)
                nc.vector.tensor_tensor_reduce(
                    out=score2[:, head, :], in0=score[:, head, :], in1=gat_count[:], scale=1.0, scalar=0.0,
                    op0=ALU.mult, op1=ALU.add, accum_out=stat[:, GAT_SUM + head:GAT_SUM + head + 1]
                    ).then_inc(s["alpha_ready"], 1)
            dve.wait_ge(s["alpha_ready"], 2 * n)
            nc.vector.reciprocal(stat[:, GAT_RCP + both[0]:GAT_RCP + both[0] + 2],
                                 stat[:, GAT_SUM + both[0]:GAT_SUM + both[0] + 2]).then_inc(s["gat_rcp"], 1)

        def gat_bank(g, half):
            return bank[((0, 1), (7, 2))[g][half]]

        def basis_product(pe, layer, it, u, half):
            slot = HALVES * u + half
            pe.wait_ge(half_in[slot], it * 16 + (layer * TILES // LOOP_TILES + 1) * 16)
            for step in range(STEPS // HALVES):
                q = half * (STEPS // HALVES) + step
                for j in range(GROUPS):
                    c = (j * (STEPS // HALVES) + step) * D
                    mm = nc.tensor.matmul(bank[u % 2][32 * j:32 * j + 32, :],
                                          att_w[:, layer, q * 32:(q + 1) * 32], ring[0:BP, slot, c:c + D],
                                          start=(q == 0), stop=(q == STEPS - 1))
            mm.then_inc(s["half_free"], 1)

        def contract(pe, layer, it, u):
            mm_tile = it * LOOP_TILES + (layer * TILES + u + 1)
            pe.wait_ge(s["w_copied"], mm_tile)
            pe.wait_ge(s["y_ready"], mm_tile)
            nc.tensor.matmul(bank[2][0:N, :], y_now[:, u, :], w_sb[:, u % 2, :], start=False, stop=True,
                             skip_group_check=True).then_inc(s["contracted"], 1)

        def open_edge_mixes(pe):
            pe.wait_ge(s["yT_ready"], 2)
            for n in range(2):
                nc.tensor.matmul(bank[6 + n][0:N, 0:EB * N], ident[0:1, 1:N + 1],
                                 ones[0:1, :].unsqueeze(1).broadcast_to([1, EB, N]), start=True, stop=True,
                                 skip_group_check=True)

        def edge_mix(pe, c, b):
            pe.wait_ge(s["hot_c_ready"], c + 1)
            pe.wait_ge(s["hot_w_ready"], c + 1)
            for n in range(2):
                mm = nc.tensor.matmul(bank[6 + n][0:N, 0:EB * N], src_c[:, b, :],
                                      work[:, b, n * EB * N:(n + 1) * EB * N], start=False, stop=True,
                                      skip_group_check=True)
            mm.then_inc(s["hot_w_used"], 1)

        def gat_vector(pe, it, u):
            nc.tensor.matmul(bank[3 + u % 2][0:N, :], pick(u, LOOP_TILES), avec_rows[:, bass.ds(it, 1), :],
                             start=True, stop=True).then_inc(s["avec_done"], 1)

        def bias_bank(g):
            return bank[(4, 3, 4, 5)[g]]

        def gat_biases(pe, gs):
            for g in gs:
                if g >= 2:
                    pe.wait_ge(s["bvec_ready"], g - 1)
                nc.tensor.matmul(bias_bank(g)[0:N, :], pick(ROW_B1 + g), rows[:], start=True, stop=True
                                 ).then_inc(s["bvec_done"], 1)

        def biases_out(act, gs):
            for g in gs:
                act.wait_ge(s["bvec_done"], g + 1)
                nc.scalar.copy(bvec[:, g // 2, (g % 2) * D:(g % 2 + 1) * D], bias_bank(g)[0:N, :]
                               ).then_inc(s["bvec_ready"], 1)

        def late_loads(sp):
            sp.dma_start(edge_i[:, 3, :], io["edge_type_8"].rearrange("(p c) -> p c", p=P)).then_inc(s["etype_in"], 16)
            sp.dma_start(weight[:], io["edge_weight"].rearrange("(p c) -> p c", p=P)).then_inc(s["weight_in"], 16)
            for layer in range(2):
                sp.dma_start(comp[:, layer, :], io[f"L3_gnn_comp{layer}"].rearrange("t b -> (t b)").partition_broadcast(P)
                              ).then_inc(s["comp_in"], 16)
            single = ((ROW_BFC, "L2_gnn_bfc"), (ROW_L3B, "L3_gnn_bias0"), (ROW_L3B + 1, "L3_gnn_bias1"))
            double = ((ROW_B1, io["L2_gnn_b1"]), (ROW_B2, io["L2_gnn_b2"]))
            for r, name in single:
                sp.dma_start(rows[r:r + 1, :], row(io[name])).then_inc(s["rows_in"], 16)
            for r, ap in double:
                sp.dma_start(rows[r:r + 2, :], ap.rearrange("(a f) -> a f", a=2)).then_inc(s["rows_in"], 16)
            sp.dma_start(root2, chunked(io["L1_gnn_root2"])).then_inc(s["root2_in"], 16)

        @block.sync
        def _(sp):
            sp.dma_start(x[:], io["x"]).then_inc(s["x_in"], 16)
            sp.dma_start(wqk[:, 0, :, :], chunked(io["L0_gnn_Wq"])[:, :, D - HD:D]).then_inc(s["wqk_in"], 16)
            sp.dma_start(wv, chunked(io["L0_gnn_Wv"])).then_inc(s["wv_in"], 16)
            sp.dma_start(wqk[:, 1, :, :], chunked(io["L0_gnn_Wk"])[:, :, D - HD:D]).then_inc(s["wqk_in"], 16)
            sp.dma_start(root1, chunked(io["L1_gnn_root1"])).then_inc(s["root1_in"], 16)
            for n, name in enumerate(("bq", "bk")):
                sp.dma_start(bqk[:, n, :], row(io[f"L0_gnn_{name}"])[:, D - HD:D]).then_inc(s["bqk_in"], 16)
            sp.dma_start(rows[ROW_BV:ROW_BV + 1, :], row(io["L0_gnn_bv"])).then_inc(s["bias_in"], 16)
            for r in range(2):
                sp.dma_start(rows[ROW_L1B + r:ROW_L1B + r + 1, :], row(io[f"L1_gnn_bias{r + 1}"])).then_inc(s["bias_in"], 16)
            for layer, basis in enumerate((io["L1_gnn_basis1"], io["L1_gnn_basis2"])):
                if layer:
                    late_loads(sp)
                view = basis.rearrange("b (t k j h q) o -> t h b k j (q o)", t=TILES, k=BLOCKS, j=GROUPS, h=HALVES)
                with sp.Fori(0, TILES // LOOP_TILES) as it:
                    for slot in range(SLOTS):
                        sp.wait_ge(s["half_free"], it * SLOTS + (layer * TILES * HALVES + slot + 1))
                        tile = view[bass.ds(it * LOOP_TILES + slot // HALVES, 1), slot % HALVES]
                        sp.dma_start(ring[0:BP, slot, :].rearrange("p (j f) -> p j f", j=GROUPS),
                                     tile.rearrange("t b k j f -> (t b) k j f")).then_inc(half_in[slot], 16)

            def slot_free(slot):
                sp.wait_ge(s["half_free"], 2 * TILES * HALVES + slot + 1)

            w1, w2 = chunked(io["L2_gnn_W1"]), chunked(io["L2_gnn_W2"])
            slot_free(0)
            sp.dma_start(W1[:, :, 0:D], w1[:, :, 0:D]).then_inc(s["w1_in"], 16)
            sp.dma_start(W1[:, :, D:GD], w1[:, :, D:GD]).then_inc(s["w1b_in"], 16)
            slot_free(1)
            sp.dma_start(W2[:, 0:4, :], w2[:, 0:4, :]).then_inc(s["w2_in"], 16)
            slot_free(2)
            sp.dma_start(W2[:, 4:8, :], w2[:, 4:8, :]).then_inc(s["w2b_in"], 16)
            slot_free(3)
            sp.dma_start(Wfc, chunked(io["L2_gnn_Wfc"])).then_inc(s["wfc_in"], 16)

            def bases(to, basis, b):
                return sp.dma_start(to, basis[b:b + 2].rearrange("b (k p) f -> p (b k) f", p=P))

            slot_free(4)
            bases(ring[:, 4, :].rearrange("p (c f) -> p c f", c=8), io["L3_gnn_basis0"], 0).then_inc(s["b0a_in"], 16)
            slot_free(5)
            bases(ring[:, 5, :].rearrange("p (c f) -> p c f", c=8), io["L3_gnn_basis0"], 2).then_inc(s["b0b_in"], 16)
            slot_free(6)
            sp.dma_start(conv_w[0][4], chunked(io["L3_gnn_loop0"])).then_inc(s["loops_in"], 16)
            sp.dma_start(conv_w[1][4], chunked(io["L3_gnn_loop1"])).then_inc(s["loops_in"], 16)
            slot_free(7)
            bases(ring[:, 7, :].rearrange("p (c f) -> p c f", c=8), io["L3_gnn_basis1"], 0).then_inc(s["b1a_in"], 16)
            sp.wait_ge(s["proj_done"], 2)
            bases(ring[:, 0, :].rearrange("p (c f) -> p c f", c=8), io["L3_gnn_basis1"], 2).then_inc(s["b1b_in"], 16)

            for part in range(2):
                cols = slice(part * GC, (part + 1) * GC)
                sp.wait_ge(s["result_ready"], part + 1)
                sp.dma_start(out[:, cols], x[:, cols]).then_inc(s["out_done"], 16)
            sp.wait_ge(s["out_done"], 32)

        @block.gpsimd
        def _(pool):
            nc.gpsimd.memset(stat[0:1, 13:14], 0.0).then_inc(s["half_free"], SLOTS)
            nc.gpsimd.memset(stat[0:1, 14:15], 0.0).then_inc(s["contracted"], LOOP_TILES)
            nc.gpsimd.memset(stat[0:1, 15:16], 0.0).then_inc(s["hot_w_used"], 2)
            nc.gpsimd.iota(iota[:], [[1, N]], base=0, channel_multiplier=0,
                           allow_small_or_imprecise_dtypes=True).then_inc(s["iota_ready"], 1)
            nc.gpsimd.memset(ident[:], 0.0).then_inc(s["ident_ready"], 1)
            pool.wait_ge(s["ident_ready"], 1)
            nc.gpsimd.affine_select(out=ident[:], in_=ident[:], compare_op=ALU.not_equal, fill=1.0, base=0,
                                    pattern=[[-1, P]], channel_multiplier=1).then_inc(s["ident_ready"], 1)
            nc.gpsimd.memset(stat[:, NEG_HALF:NEG_HALF + 1], -0.5).then_inc(s["consts_ready"], 1)
            nc.gpsimd.memset(ones[:], 1.0).then_inc(s["consts_ready"], 1)
            nc.gpsimd.memset(uniform[:], 1.0 / N).then_inc(s["consts_ready"], 1)

            rstd_pow(pool, 1)

            nc.gpsimd.memset(mixed[:], 0.0).then_inc(s["mixed_zero"], 1)
            rstd_pow(pool, 2)

            pool.wait_ge(s["coef_ready"], 1)
            pool.wait_ge(s["avec_done"], 8)
            with pool.Fori(0, EC // 2) as it:
                for b in range(2):
                    pool.wait_ge(s["hot_w_used"], it * 2 + (b + 1))
                    nc.gpsimd.tensor_copy(src_c[:, b:b + 1, :], src_hot[:, bass.ds(it * 2 + b, 1), :]
                                          ).then_inc(s["hot_c_ready"], 1)
                    nc.gpsimd.tensor_tensor(
                        work[:, b, :].rearrange("p (c n) -> p c n", n=N),
                        dst_hot[:, bass.ds(it * 2 + b, 1), :].broadcast_to([P, 2 * EB, N]),
                        coef[:, bass.ds(it * 2 + b, 1), :, :].rearrange("p e l b -> p (e l b)").unsqueeze(2)
                        .broadcast_to([P, 2 * EB, N]),
                        ALU.mult).then_inc(s["hot_w_ready"], 1)
            rstd_pow(pool, 3)
            rstd_pow(pool, 4)

        @block.scalar
        def _(act):
            for n, name in enumerate(("src", "dst")):
                act.dma_start(edge_i[:, n, :], io[name].rearrange("(p c) -> p c", p=P)).then_inc(s["edges_in"], 16)
            act.dma_start(edge_i[:, 2, :], io["edge_type_2"].rearrange("(p c) -> p c", p=P)).then_inc(s["rel_in"], 16)

            for layer in range(2):
                act.dma_start(att_rows[layer * NR:(layer + 1) * NR, :], io[f"L1_gnn_att{layer + 1}"]
                              ).then_inc(s["att_in"], 16)
                act.dma_start(gate_rows[layer * NR:(layer + 1) * NR, :],
                              io[f"L1_gnn_gate_w{layer + 1}"].rearrange("r f a -> r (f a)")).then_inc(s["gate_in"], 16)
            for n, name in enumerate(("a_src1", "a_dst1", "a_src2", "a_dst2")):
                act.dma_start(avec_rows[n % 2 * 2:n % 2 * 2 + 2, n // 2, :],
                              io[f"L2_gnn_{name}"].rearrange("g c -> (g c)").rearrange("(a f) -> a f", a=2)
                              ).then_inc(s["avec_in"], 16)
            act.wait_ge(s["qk_done"], 1)
            nc.scalar.copy(qk, bank[5][0:HD, 0:2 * N].rearrange("p (a n) -> p a n", a=2)).then_inc(s["qk_ready"], 1)
            act.wait_ge(s["v_done"], 1)
            nc.scalar.copy(v, bank[6][0:N, :]).then_inc(s["v_ready"], 1)
            act.wait_ge(s["max_ready"], 1)
            nc.scalar.activation(score[:, 1, :], score[:, 0, :], ACT.Exp, bias=stat[:, NEG_MAX:NEG_MAX + 1],
                                 accum_out=stat[:, EXP_SUM:EXP_SUM + 1]).then_inc(s["exp_ready"], 1)

            for layer in range(2):
                act.wait_ge(s["gates_done"], layer + 1)
                nc.scalar.activation(z_exp[:], bank[4][0:N, 0:NR], ACT.Exp, scale=-1.0).then_inc(s["z_ready"], 1)
                act.wait_ge(s["yT_done"], 2 * layer + 1)
                if layer:
                    act.wait_ge(s["y_ready"], TILES)
                nc.scalar.copy(yT[:, 0:4, :], bank[5][:, 0:4 * N].rearrange("p (t n) -> p t n", t=4)
                               ).then_inc(s["yT_a"], 1)
                if layer:
                    biases_out(act, range(0, 2))
                with act.Fori(0, TILES // LOOP_TILES) as it:
                    for u in range(LOOP_TILES):
                        act.wait_ge(s["half_free"], it * SLOTS + (SLOTS + HALVES * (layer * TILES + u + 1)))
                        nc.scalar.copy(w_sb[:, u % 2, :], bank[u % 2][:]).then_inc(s["w_copied"], 1)
                        if layer == 0:
                            act.wait_ge(s["avec_done"], it * LOOP_TILES + (u + 1))
                            nc.scalar.copy(early[0:N, :].rearrange("p (g f) -> p g f", g=8)
                                           [:, bass.ds(it * LOOP_TILES + u, 1), :],
                                           bank[3 + u % 2][0:N, :].unsqueeze(1)).then_inc(s["avec_ready"], 1)

            biases_out(act, range(2, 4))
            for g in range(2):
                for half in range(2):
                    n = 2 * g + half + 1
                    heads = slice(2 * half, 2 * half + 2)
                    if half:
                        copy_low(act, g)
                    for m, head in enumerate((2 * half, 2 * half + 1)):
                        act.wait_ge(s["s_masked"], 2 * (n - 1) + m + 1)
                        nc.scalar.activation(score[:, head, :], score[:, head, :], ACT.Exp, scale=-1.0,
                                             bias=stat[:, GAT_MAX + head:GAT_MAX + head + 1]).then_inc(s["s_exp"], 1)
                    act.wait_ge(s["alpha_turned"], n)
                    nc.scalar.copy(alphaT[:, heads, :],
                                   bank[6][0:N, 2 * half * N:(2 * half + 2) * N].rearrange("p (g n) -> p g n", g=2)
                                   ).then_inc(s["alphaT_ready"], 1)
                    act.wait_ge(s["gat_rcp"], n)
                    if half == 0:
                        act.wait_ge(s["gat_out"], 3 * g + 1)
                        for head in (0, 1):
                            evacuate(nc.scalar, head).then_inc(s["gat_low_ready"], 1)
                    else:
                        act.wait_ge(s["gat_out"], 3 * g + 3)
                        evacuate(nc.scalar, 3).then_inc(s["gat_h3_ready"], 1)
            for layer in range(2):
                for k in (1, 3):
                    act.wait_ge(s["zT_done"], layer * KC + k + 1)
                    nc.scalar.copy(zT[:, k, :], bank[3 + k][:, 0:5 * N]).then_inc(s["zT_act"], 1)

        @block.vector
        def _(dve):
            def norm_stats(part):
                nc.vector.bn_stats(stat[:, BN + 6 * part:BN + 6 * part + 6], x[:, part * GC:(part + 1) * GC]
                                   ).then_inc(s["ln_stats"], 1)

            def layer_norm(n):
                dve.wait_ge(s["ln_stats"], 3 * n - 1)
                nc.vector.bn_aggr(stat[:, MEAN:MEAN + 2], stat[:, BN:BN + 12]).then_inc(s["ln_stats"], 1)
                dve.wait_ge(s["ln_stats"], 3 * n)
                nc.vector.tensor_scalar(stat[:, VAR_EPS:VAR_EPS + 1], stat[:, VAR:VAR + 1], EPS, None, ALU.add
                                        ).then_inc(s["ln_var"], 1)
                nc.vector.tensor_scalar(h[:], x[:], stat[:, MEAN:MEAN + 1], 0.0, ALU.subtract, ALU.max
                                        ).then_inc(s["ln_centred"], 1)
                dve.wait_ge(s["ln_centred"], n)
                dve.wait_ge(s["ln_rstd"], n)
                nc.vector.tensor_scalar(h[:], h[:], stat[:, RSTD:RSTD + 1], None, ALU.mult).then_inc(s["h_ready"], 1)

            def copy_hT(n):
                dve.wait_ge(s["hT_done"], n)
                nc.vector.tensor_copy(hT[:, 0:4, :], bank[3][:, 0:4 * N].rearrange("p (k n) -> p k n", k=4)
                                      ).then_inc(s["hT_ready"], 1)

            dve.wait_ge(s["x_in"], 16)
            for part in range(2):
                norm_stats(part)
            layer_norm(1)
            dve.wait_ge(s["edges_in"], 32)
            nc.vector.tensor_copy(edge_f[:, 0:2, :], edge_i[:, 0:2, :]).then_inc(s["edges_float"], 1)
            dve.wait_ge(s["rel_in"], 16)
            nc.vector.tensor_copy(edge_f[:, 2, :], edge_i[:, 2, :]).then_inc(s["edges_float"], 1)
            dve.wait_ge(s["edges_float"], 2)
            nc.vector.tensor_scalar(is_rel0[:], edge_f[:, 2, :], 0.0, None, ALU.is_equal).then_inc(s["edges_float"], 1)

            dve.wait_ge(s["iota_ready"], 1)
            every_node = iota[:].unsqueeze(1).broadcast_to([P, EC, N])
            for n, hot in enumerate((src_hot, dst_hot)):
                nc.vector.tensor_tensor(hot, edge_f[:, n, :].unsqueeze(2).broadcast_to([P, EC, N]), every_node,
                                        ALU.is_equal).then_inc(s["hots_ready"], 1)
            dve.wait_ge(s["edges_float"], 3)
            dve.wait_ge(s["hots_ready"], 2)
            nc.vector.tensor_tensor(src_hot0, src_hot, is_rel0[:].unsqueeze(2).broadcast_to([P, EC, N]),
                                    ALU.mult).then_inc(s["hot0_ready"], 1)
            dve.wait_ge(s["ident_ready"], 2)
            nc.vector.tensor_reduce(same_block[:], ident[0:BP, 0:BP].rearrange("p (b k) -> p k b", k=BLOCKS), X, ALU.add
                                    ).then_inc(s["block_ready"], 1)
            nc.vector.memset(att_w[:], 0.0).then_inc(s["attw_zero"], 1)
            copy_hT(1)

            dve.wait_ge(s["counts_done"], 1)
            nc.vector.tensor_scalar(has_edge[:], bank[4][0:N, 0:N], 0.0, None, ALU.is_gt).then_inc(s["edge_mask"], 1)
            nc.vector.tensor_copy(relT[:, 0, :], bank[4][0:N, 2 * N:3 * N]).then_inc(s["rel_ready"], 1)
            nc.vector.tensor_tensor(gat_count[:], bank[4][0:N, N:2 * N], ident[0:N, 0:N], ALU.add
                                    ).then_inc(s["gat_mask"], 1)
            dve.wait_ge(s["rel_ready"], 1)
            nc.vector.tensor_tensor(relT[:, 1, :], bank[4][0:N, N:2 * N], relT[:, 0, :], ALU.subtract
                                    ).then_inc(s["rel_ready"], 1)
            dve.wait_ge(s["gat_mask"], 1)
            nc.vector.tensor_scalar(absent[:], gat_count[:], 0.0, ABSENT, ALU.is_equal, ALU.mult
                                    ).then_inc(s["gat_mask"], 1)

            dve.wait_ge(s["att_in"], 32)
            nc.vector.tensor_copy(expand, att_rows[:].unsqueeze(2).broadcast_to([2 * NR, NB, BLOCKS])
                                  ).then_inc(s["expand_ready"], 1)

            dve.wait_ge(s["scores_done"], 1)
            dve.wait_ge(s["edge_mask"], 1)
            nc.vector.scalar_tensor_tensor(out=score[:, 0, :], in0=bank[7][0:N, 0:N], scalar=float(HD) ** -0.5,
                                           in1=has_edge[:], op0=ALU.mult, op1=ALU.mult).then_inc(s["masked"], 1)
            dve.wait_ge(s["masked"], 1)
            nc.vector.tensor_reduce(stat[:, NEG_MAX:NEG_MAX + 1], score[:, 0, :], X, ALU.max, negate=True
                                    ).then_inc(s["max_ready"], 1)
            dve.wait_ge(s["exp_ready"], 1)
            nc.vector.reciprocal(stat[:, EXP_RCP:EXP_RCP + 1], stat[:, EXP_SUM:EXP_SUM + 1]).then_inc(s["masked"], 1)
            dve.wait_ge(s["masked"], 2)
            nc.vector.tensor_scalar(score[:, 1, :], score[:, 1, :], stat[:, EXP_RCP:EXP_RCP + 1], None, ALU.mult
                                    ).then_inc(s["att_norm"], 1)
            dve.wait_ge(s["att_turned"], 1)
            nc.vector.tensor_copy(alphaT[:, 0, :], bank[3][0:N, 0:N]).then_inc(s["att_turned_ready"], 1)
            dve.wait_ge(s["attn_done"], 1)
            nc.vector.tensor_tensor(x[:], x[:], bank[5][0:N, :], ALU.add).then_inc(s["x_ready"], 1)
            dve.wait_ge(s["x_ready"], 1)
            for part in range(2):
                norm_stats(part)
            layer_norm(2)

            dve.wait_ge(s["attp_done"], 1)
            nc.vector.tensor_copy(att_p[:], bank[7][0:BP, 0:2 * NR]).then_inc(s["attp_ready"], 1)
            dve.wait_ge(s["attp_ready"], 1)
            dve.wait_ge(s["block_ready"], 1)
            dve.wait_ge(s["attw_zero"], 1)
            for layer in range(2):
                for r in range(NR):
                    nc.vector.tensor_scalar(
                        att_w[:, layer, :].rearrange("p (q c) -> p q c", q=STEPS)[:, :, 4 * r:4 * r + 4],
                        same_block[:].unsqueeze(1).broadcast_to([BP, STEPS, BLOCKS]),
                        att_p[:, layer * NR + r:layer * NR + r + 1], None, ALU.mult).then_inc(s["attw_ready"], 1)
            dve.wait_ge(s["gateT_done"], 1)
            nc.vector.tensor_copy(gateT[:], bank[6][:, 0:KC * 2 * NR].rearrange("p (k g) -> p k g", k=KC)
                                  ).then_inc(s["gateT_ready"], 1)

            for layer in range(2):
                copy_hT(2 + layer)
                dve.wait_ge(s["z_ready"], layer + 1)
                nc.vector.tensor_scalar(gate[:], z_exp[:], 1.0, None, ALU.add).then_inc(s["gate_p1"], 1)
                dve.wait_ge(s["gate_p1"], layer + 1)
                nc.vector.reciprocal(gate[:], gate[:]).then_inc(s["gate_ready"], 1)
                dve.wait_ge(s["gate_ready"], layer + 1)
                dve.wait_ge(s["mixed_zero"], 1)
                for r in range(NR):
                    nc.vector.tensor_scalar(
                        mixed[:, r, :].rearrange("p (t s r k) -> p t s r k", t=TILES, r=NR, k=BLOCKS)[:, :, :, r, :],
                        h[:].rearrange("p (t k s) -> p t s k", t=TILES, k=BLOCKS),
                        gate[:, r:r + 1], None, ALU.mult).then_inc(s["mixed_ready"], 1)
                dve.wait_ge(s["yT_done"], 2 * layer + 2)
                nc.vector.tensor_copy(yT[:, 4:8, :], bank[6][:, 0:4 * N].rearrange("p (t n) -> p t n", t=4)
                                      ).then_inc(s["yT_ready"], 1)
                if layer:
                    edge_coefficients(dve)
                dve.wait_ge(s["yT_a"], layer + 1)
                dve.wait_ge(s["yT_ready"], layer + 1)
                with dve.Fori(0, TILES // LOOP_TILES) as it:
                    for u in range(LOOP_TILES):
                        dve.wait_ge(s["contracted"], it * LOOP_TILES + (layer * TILES + u + 1))
                        nc.vector.tensor_copy(y_now[:, u:u + 1, :], yT[:, bass.ds(it * LOOP_TILES + u, 1), :]
                                              ).then_inc(s["y_ready"], 1)
                dve.wait_ge(s["contracted"], LOOP_TILES + (layer + 1) * TILES)
                if layer == 0:
                    nc.vector.tensor_scalar(h[:], bank[2][0:N, :], 0.0, None, ALU.max).then_inc(s["h_ready"], 1)
                else:
                    nc.vector.tensor_tensor(x[:], x[:], bank[2][0:N, :], ALU.add).then_inc(s["x_ready"], 1)
                    dve.wait_ge(s["x_ready"], 2)
                    for part in range(2):
                        norm_stats(part)
                    layer_norm(3)

            for g in range(2):
                if g == 0:
                    copy_hT(4)
                    for n in range(2):
                        dve.wait_ge(s["hot_w_used"], 2 + EC)
                        nc.vector.tensor_copy(mix3[:, n, 0:EB * N], bank[6 + n][0:N, 0:EB * N]).then_inc(s["mix_ready"], 1)
                        nc.vector.tensor_copy(mix3[:, n, EB * N:], ident[0:N, 0:N]).then_inc(s["mix_ready"], 1)
                for half in range(2):
                    gat_softmax(dve, g, half)
                dve.wait_ge(s["gat_rcp"], 2 * g + 2)
                dve.wait_ge(s["gat_out"], 3 * g + 2)
                evacuate(nc.vector, 2).then_inc(s["gat_h2_ready"], 1)
                dve.wait_ge(s["high_done"], g + 1)
                nc.vector.tensor_copy(hT[:, 4:8, :], bank[3][:, 0:4 * N].rearrange("p (k n) -> p k n", k=4)
                                      ).then_inc(s["high_ready"], 1)

            for part in range(2):
                cols = slice(part * GC, (part + 1) * GC)
                dve.wait_ge(s["fc_done"], part + 1)
                nc.vector.tensor_tensor(x[:, cols], x[:, cols], bank[part][0:N, 0:GC], ALU.add).then_inc(s["x_ready"], 1)
                dve.wait_ge(s["x_ready"], 3 + part)
                norm_stats(part)
            layer_norm(4)
            for layer in range(2):
                for k in (0, 2):
                    dve.wait_ge(s["zT_done"], layer * KC + k + 1)
                    nc.vector.tensor_copy(zT[:, k, :], bank[3 + k][:, 0:5 * N]).then_inc(s["zT_dve"], 1)
                dve.wait_ge(s["conv_done"], layer + 1)
                if layer == 0:
                    nc.vector.tensor_scalar(h[:], bank[7][0:N, :], 0.0, None, ALU.max).then_inc(s["h_ready"], 1)
                else:
                    for part in range(2):
                        cols = slice(part * GC, (part + 1) * GC)
                        dve.wait_ge(s["conv_done"], 2 + part)
                        nc.vector.tensor_tensor(x[:, cols], x[:, cols], bank[(2, 1)[part]][0:N, 0:GC], ALU.add
                                                ).then_inc(s["result_ready"], 1)

        @block.tensor
        def _(pe):
            def transposes(source, n, to, done):
                for k in range(4):
                    c = (n + k) * P
                    mm = nc.tensor.transpose(to[:, k * N:(k + 1) * N], source[:, c:c + P], ident[0:N, 0:N])
                mm.then_inc(s[done], 1)

            pe.wait_ge(s["ident_ready"], 2)
            pe.wait_ge(s["h_ready"], 1)
            transposes(h, 0, bank[3], "hT_done")
            pe.wait_ge(s["hT_ready"], 1)
            pe.wait_ge(s["wqk_in"], 32)
            pe.wait_ge(s["bqk_in"], 32)
            pe.wait_ge(s["consts_ready"], 3)
            for n in range(2):
                q_ps = bank[5][0:HD, n * N:(n + 1) * N]
                nc.tensor.matmul(q_ps, bqk[:, n, :], ones[0:1, :], start=True, stop=False)
                for k in range(KC):
                    mm = nc.tensor.matmul(q_ps, wqk[:, n, k, :], hT[:, k, :], start=False, stop=(k == KC - 1))
            mm.then_inc(s["qk_done"], 1)
            pe.wait_ge(s["hots_ready"], 2)
            pe.wait_ge(s["hot0_ready"], 1)
            for n, (left, right) in enumerate(((src_hot, dst_hot), (dst_hot, src_hot), (dst_hot, src_hot0))):
                for c in range(EC):
                    mm = nc.tensor.matmul(bank[4][0:N, n * N:(n + 1) * N], left[:, c, :], right[:, c, :],
                                          start=(c == 0), stop=(c == EC - 1))
            mm.then_inc(s["counts_done"], 1)
            pe.wait_ge(s["qk_ready"], 1)
            nc.tensor.matmul(bank[7][0:N, 0:N], qk[:, 0, :], qk[:, 1, :], start=True, stop=True).then_inc(s["scores_done"], 1)
            pe.wait_ge(s["bias_in"], 48)
            nc.tensor.matmul(bank[6][0:N, :], ones[0:1, :], rows[0:1, :], start=True, stop=False)
            pe.wait_ge(s["wv_in"], 16)
            for k in range(KC):
                mm = nc.tensor.matmul(bank[6][0:N, :], hT[:, k, :], wv[:, k, :], start=False, stop=(k == KC - 1))
            mm.then_inc(s["v_done"], 1)
            pe.wait_ge(s["v_ready"], 1)
            pe.wait_ge(s["gate_in"], 32)
            for k in range(KC):
                mm = nc.tensor.transpose(bank[6][:, k * 2 * NR:(k + 1) * 2 * NR], gate_rows[:, k * P:(k + 1) * P],
                                         ident[0:2 * NR, 0:2 * NR])
            mm.then_inc(s["gateT_done"], 1)
            pe.wait_ge(s["att_norm"], 1)
            nc.tensor.transpose(bank[3][0:N, 0:N], score[:, 1, :], ident[0:N, 0:N]).then_inc(s["att_turned"], 1)
            pe.wait_ge(s["expand_ready"], 1)
            nc.tensor.transpose(bank[7][0:BP, 0:2 * NR], expand.rearrange("p b k -> p (b k)"),
                                ident[0:2 * NR, 0:2 * NR]).then_inc(s["attp_done"], 1)
            pe.wait_ge(s["att_turned_ready"], 1)
            nc.tensor.matmul(bank[5][0:N, 0:D - HD], uniform[:], v[:, 0:D - HD], start=True, stop=True)
            nc.tensor.matmul(bank[5][0:N, D - HD:D], alphaT[:, 0, :], v[:, D - HD:D], start=True, stop=True
                             ).then_inc(s["attn_done"], 1)

            for layer in range(2):
                pe.wait_ge(s["h_ready"], 2 + layer)
                transposes(h, 0, bank[3], "hT_done")
                pe.wait_ge(s["hT_ready"], 2 + layer)
                pe.wait_ge(s["gateT_ready"], 1)
                pe.wait_ge(s["gat_mask"], 2)
                for k in range(KC):
                    mm = nc.tensor.matmul(bank[4][0:N, 0:NR], hT[:, k, :], gateT[:, k, layer * NR:(layer + 1) * NR],
                                          start=(k == 0), stop=(k == KC - 1))
                mm.then_inc(s["gates_done"], 1)
                pe.wait_ge(s["bias_in"], 48)
                nc.tensor.matmul(bank[2][0:N, :], pick(ROW_L1B + layer, ROW_B1), rows[0:ROW_B1, :], start=True, stop=True,
                                 skip_group_check=True)
                pe.wait_ge(s[f"root{layer + 1}_in"], 16)
                root = (root1, root2)[layer]
                for k in range(KC):
                    nc.tensor.matmul(bank[2][0:N, :], hT[:, k, :], root[:, k, :], start=False, stop=True,
                                     skip_group_check=True)
                pe.wait_ge(s["mixed_ready"], 2 * (layer + 1))
                pe.wait_ge(s["rel_ready"], 2)
                for t in range(TILES):
                    y_ps = bank[5 + t // 4][:, (t % 4) * N:(t % 4 + 1) * N]
                    for r in range(NR):
                        mm = nc.tensor.matmul(y_ps, mixed[:, r, t * P:(t + 1) * P], relT[:, r, :],
                                              start=(r == 0), stop=(r == NR - 1))
                    if t % 4 == 3:
                        mm.then_inc(s["yT_done"], 1)
                pe.wait_ge(s["attw_ready"], 4)
                if layer == 0:
                    pe.wait_ge(s["avec_in"], 64)
                else:
                    pe.wait_ge(s["rows_in"], 16 * 5)
                    gat_biases(pe, range(0, 2))
                    open_edge_mixes(pe)
                rounds = TILES // LOOP_TILES
                mixes = ((0,), (1, 2), (3,), (4,))
                with pe.Fori(0, rounds) as it:
                    for u in range(LOOP_TILES):
                        basis_product(pe, layer, it, u, 0)
                        if u:
                            contract(pe, layer, it, u - 1)
                        if layer == 0:
                            gat_vector(pe, it, u)
                        else:
                            for n in mixes[u]:
                                edge_mix(pe, it * (EC // rounds) + n, n % 2)
                        basis_product(pe, layer, it, u, 1)
                    contract(pe, layer, it, LOOP_TILES - 1)
                    if layer:
                        edge_mix(pe, it * (EC // rounds) + EC // rounds - 1, 1)
                if layer == 0:
                    pe.wait_ge(s["avec_ready"], 8)

            def keep_clock(n, b):
                for _ in range(n):
                    nc.tensor.matmul(bank[b][0:N, :], src_hot[:, 0, :], hots[:, 1].rearrange("p e n -> p (e n)")[:, 0:D],
                                     start=True, stop=True)

            def proj(g, half, k):
                last = (3, 7)[g]
                mm = nc.tensor.matmul(gat_bank(g, half)[0:N, :], hT[:, k, :], (W1, W2)[g][:, k, half * D:(half + 1) * D],
                                      start=(k == 0), stop=(k == last))
                if k == last:
                    mm.then_inc(s["proj_done"], 1)

            def fc(part, k):
                cols = slice(part * GC, (part + 1) * GC)
                mm = nc.tensor.matmul(bank[part][0:N, 0:GC], hT[:, k, :], Wfc[:, k, cols], start=False, stop=(k == 7))
                if k == 7:
                    mm.then_inc(s["fc_done"], 1)

            def turn_low(g):
                pe.wait_ge(s["gat_low_ready"], 2 * (g + 1))
                transposes(gat_o, 0, bank[3], "low_done")

            def turn_high(g):
                pe.wait_ge(s["gat_h2_ready"], g + 1)
                pe.wait_ge(s["gat_h3_ready"], g + 1)
                transposes(gat_o, 4, bank[3], "high_done")

            def source_scores(g, half):
                n = 2 * g + half + 1
                pe.wait_ge(s["diag_ready"], n)
                nc.tensor.matmul(bank[5][0:N, 2 * half * N:(2 * half + 2) * N], ones[:],
                                 score[:, 2 * half:2 * half + 2, :].rearrange("p g n -> p (g n)"),
                                 start=True, stop=True).then_inc(s["e_done"], 1)

            def turn_weights(g, half):
                for head in (2 * half, 2 * half + 1):
                    pe.wait_ge(s["alpha_ready"], 4 * g + head + 1)
                    mm = nc.tensor.transpose(bank[6][0:N, head * N:(head + 1) * N], score2[:, head, :], ident[0:N, 0:N])
                mm.then_inc(s["alpha_turned"], 1)

            def weigh(g, half):
                pe.wait_ge(s["alphaT_ready"], 2 * g + half + 1)
                pe.wait_ge(s["gat_h_ready"], 2 * g + half + 1)
                if half:
                    pe.wait_ge(s["gat_low_ready"], 2 * (g + 1))
                for head in (2 * half, 2 * half + 1):
                    ps = (bank[4], bank[4], bank[4], bank[5])[head]
                    mm = nc.tensor.matmul(ps[0:N, head % 2 * GC:(head % 2 + 1) * GC], alphaT[:, head, :],
                                          gat_h[:, head * GC:(head + 1) * GC], start=True, stop=True)
                    if head:
                        mm.then_inc(s["gat_out"], 1)

            gat_biases(pe, range(2, 4))
            pe.wait_ge(s["h_ready"], 4)
            transposes(h, 0, bank[3], "hT_done")
            keep_clock(3, 2)
            pe.wait_ge(s["hT_ready"], 4)
            pe.wait_ge(s["w1_in"], 16)
            for k in range(4):
                proj(0, 0, k)
            pe.wait_ge(s["w1b_in"], 16)
            proj(0, 1, 0)
            proj(0, 1, 1)
            pe.wait_ge(s["bvec_ready"], 4)
            source_scores(0, 0)
            proj(0, 1, 2)
            proj(0, 1, 3)
            keep_clock(2, 2)
            turn_weights(0, 0)
            keep_clock(2, 2)
            weigh(0, 0)
            source_scores(0, 1)
            keep_clock(3, 2)
            turn_low(0)
            keep_clock(3, 2)
            pe.wait_ge(s["low_ready"], 1)
            pe.wait_ge(s["w2_in"], 16)
            pe.wait_ge(s["mix_ready"], 4)
            proj(1, 0, 0)
            turn_weights(0, 1)
            proj(1, 0, 1)
            weigh(0, 1)
            proj(1, 0, 2)
            proj(1, 0, 3)
            turn_high(0)
            proj(1, 1, 0)
            pe.wait_ge(s["high_ready"], 1)
            pe.wait_ge(s["w2b_in"], 16)
            for k in range(4, 8):
                proj(1, 0, k)
            for k in range(1, 8):
                if k == 3:
                    source_scores(1, 0)
                if k == 6:
                    turn_weights(1, 0)
                if k == 7:
                    weigh(1, 0)
                proj(1, 1, k)
            turn_low(1)
            for part in range(2):
                nc.tensor.matmul(bank[part][0:N, 0:GC], pick(ROW_BFC), rows[:, part * GC:(part + 1) * GC],
                                 start=True, stop=False)
            source_scores(1, 1)
            pe.wait_ge(s["low_ready"], 2)
            pe.wait_ge(s["wfc_in"], 16)
            for k in range(4):
                if k == 3:
                    turn_weights(1, 1)
                for part in range(2):
                    fc(part, k)
            weigh(1, 1)
            keep_clock(3, 2)
            turn_high(1)
            keep_clock(3, 2)
            pe.wait_ge(s["high_ready"], 2)
            for part in range(2):
                for k in range(4, 8):
                    fc(part, k)

            for layer in range(2):
                parts = (((bank[7], slice(0, D)),), ((bank[2], slice(0, GC)), (bank[1], slice(GC, D))))[layer]
                for ps, cols in parts:
                    nc.tensor.matmul(ps[0:N, 0:D // len(parts)], pick(ROW_L3B + layer), rows[:, cols],
                                     start=True, stop=False)
                if layer == 0:
                    keep_clock(8, 2)
                pe.wait_ge(s["h_ready"], 5 + layer)
                pe.wait_ge(s["mix_ready"], 4)
                for k in range(KC):
                    nc.tensor.matmul(bank[3 + k][:, 0:5 * N], h[:, k * P:(k + 1) * P], mix3[:, layer, :],
                                     start=True, stop=True).then_inc(s["zT_done"], 1)
                for name in (("b0a_in", "b0b_in"), ("b1a_in", "b1b_in"))[layer]:
                    pe.wait_ge(s[name], 16)
                pe.wait_ge(s["loops_in"], 32)
                for part, (ps, cols) in enumerate(parts):
                    for k in range(KC):
                        pe.wait_ge(s[("zT_dve", "zT_act")[k % 2]], 2 * layer + k // 2 + 1)
                        for b in range(EB + 1):
                            mm = nc.tensor.matmul(ps[0:N, 0:D // len(parts)], zT[:, k, b * N:(b + 1) * N],
                                                  conv_w[layer][b][:, k, cols], start=False,
                                                  stop=(k == KC - 1 and b == EB))
                    mm.then_inc(s["conv_done"], 1)


_OUTS = [((N, D), "float32")]


def kernel(**inputs):
    import numpy as _np
    import concourse.bacc as _bacc
    from concourse import mybir as _mybir
    from concourse.bass_utils import run_bass_kernel_spmd as _run

    nc = _bacc.Bacc("TRN2", target_bir_lowering=False, num_devices=1)
    arrays, io = {}, {}
    for name in inputs:
        a = _np.ascontiguousarray(inputs[name])
        arrays[f"in_{name}_dram"] = a
        io[name] = nc.dram_tensor(f"in_{name}_dram", a.shape, _mybir.dt.from_np(a.dtype), kind="ExternalInput").ap()
    shape, dtype = _OUTS[0]
    result = nc.dram_tensor("out_0_dram", shape, _mybir.dt.from_np(_np.dtype(dtype)), kind="ExternalOutput").ap()
    gnn_blocks(nc, io, result)
    r = _run(nc, [arrays], core_ids=[0])
    return r.results[0]["out_0_dram"]
```
